# Optimizing a Trainium2 kernel written in Bass

```python
import numpy as np
import jax
import jax.numpy as jnp

def _softmax(x, axis=-1):
    return jax.nn.softmax(x, axis=axis)

def _gelu(x):
    return jax.nn.gelu(x, approximate=True)

def _silu(x):
    return jax.nn.silu(x)

def _sigmoid(x):
    return jax.nn.sigmoid(x)

def _layernorm(x, axis=-1, eps=1e-05):
    m = jnp.mean(x, axis=axis, keepdims=True)
    v = jnp.var(x, axis=axis, keepdims=True)
    return (x - m) / jnp.sqrt(v + eps)

def _scatter_add(tgt, idx, src, axis=0):
    return tgt.at[idx].add(src)

def _segment_sum(src, seg, n):
    return jax.ops.segment_sum(src, seg, n)
kernel_name = 'mk_adj_preln_d2_adj_r2_d2f1ac'

def setup_inputs(seed: int=0):
    np.random.seed(seed)
    _w = jnp.asarray

    def _rec_inputs():
        import jax
        import jax.numpy as jnp
        _gk = jax.random.key(seed)
        x = -0.000929 + 1 * jax.random.normal(jax.random.fold_in(_gk, 1), (8192, 128), jnp.float32)
        _a = jax.random.bernoulli(jax.random.fold_in(_gk, 2), 0.000976562, (8192, 8192))
        adj = _a.astype(jnp.int32)
        return (x, adj)
    x, adj = _rec_inputs()

    def _L0_gnn_setup():
        import jax, jax.numpy as jnp
        import numpy as np
        N = 4096
        D_IN = 128
        D_OUT = 128
        ALPHA = 0.2
        NEG = -9000000000000000.0
        key = jax.random.key(seed)
        k1, k2, k3, k4 = jax.random.split(key, 4)
        input = jax.random.normal(k1, (N, D_IN), dtype=jnp.float32)
        adj = jax.random.randint(k2, (N, N), 0, 2, dtype=jnp.int32)
        lim_w = 1.414 * np.sqrt(6.0 / (D_IN + D_OUT))
        W = jax.random.uniform(k3, (D_IN, D_OUT), jnp.float32, -lim_w, lim_w)
        lim_a = 1.414 * np.sqrt(6.0 / (2 * D_OUT + 1))
        a = jax.random.uniform(k4, (2 * D_OUT, 1), jnp.float32, -lim_a, lim_a)
        return {'input': input, 'adj': adj, 'W': W, 'a': a}
    _L0_gnn_all = _L0_gnn_setup()
    _L0_gnn_in = {k: v for k, v in _L0_gnn_all.items() if k in ('W', 'a')}
    del _L0_gnn_all

    def _L1_gnn_setup():
        import jax, jax.numpy as jnp
        import numpy as np
        N = 4096
        IN_F = 128
        OUT_F = 128
        ALPHA = 0.2
        NEG_INF = -9000000000000000.0
        key = jax.random.key(seed)
        k1, k2, k3, k4 = jax.random.split(key, 4)
        h = jax.random.normal(k1, (N, IN_F), dtype=jnp.float32)
        adj = jax.random.randint(k2, (N, N), 0, 2, dtype=jnp.int32)
        W = jax.random.normal(k3, (IN_F, OUT_F), dtype=jnp.float32) * (1.0 / np.sqrt(IN_F))
        limit = 1.414 * np.sqrt(6.0 / (2 * OUT_F + 1))
        a = jax.random.uniform(k4, (2 * OUT_F, 1), dtype=jnp.float32, minval=-limit, maxval=limit)
        return {'h': h, 'adj': adj, 'W': W, 'a': a}
    _L1_gnn_all = _L1_gnn_setup()
    _L1_gnn_in = {k: v for k, v in _L1_gnn_all.items() if k in ('W', 'a')}
    del _L1_gnn_all
    return {'x': x, 'adj': adj, 'L0_gnn_W': _L0_gnn_in['W'], 'L0_gnn_a': _L0_gnn_in['a'], 'L1_gnn_W': _L1_gnn_in['W'], 'L1_gnn_a': _L1_gnn_in['a']}

def reference(x, adj, L0_gnn_W, L0_gnn_a, L1_gnn_W, L1_gnn_a):
    import jax
    import jax.numpy as jnp

    def _L0_gnn_ref(input, adj, W, a):
        import jax, jax.numpy as jnp
        import numpy as np
        N = 4096
        D_IN = 128
        D_OUT = 128
        ALPHA = 0.2
        NEG = -9000000000000000.0
        h = input @ W
        a1 = a[:D_OUT, 0]
        a2 = a[D_OUT:, 0]
        e = (h @ a1)[:, None] + (h @ a2)[None, :]
        e = jnp.where(e > 0, e, ALPHA * e)
        e = jnp.where(adj > 0, e, NEG)
        attention = jax.nn.softmax(e, axis=1)
        h_prime = attention @ h
        return jax.nn.elu(h_prime)

    def _L1_gnn_ref(h, adj, W, a):
        import jax, jax.numpy as jnp
        import numpy as np
        N = 4096
        IN_F = 128
        OUT_F = 128
        ALPHA = 0.2
        NEG_INF = -9000000000000000.0
        Wh = h @ W
        a1 = a[:OUT_F, 0]
        a2 = a[OUT_F:, 0]
        s1 = Wh @ a1
        s2 = Wh @ a2
        e = jax.nn.leaky_relu(s1[:, None] + s2[None, :], negative_slope=ALPHA)
        masked = jnp.where(adj > 0, e, NEG_INF)
        attention = jax.nn.softmax(masked, axis=1)
        h_prime = attention @ Wh
        return jax.nn.elu(h_prime)
    h = jnp.maximum(_layernorm(x, axis=-1), 0.0)
    x = x + _L0_gnn_ref(h, adj, L0_gnn_W, L0_gnn_a)
    h = jnp.maximum(_layernorm(x, axis=-1), 0.0)
    x = x + _L1_gnn_ref(h, adj, L1_gnn_W, L1_gnn_a)
    return x

_drawn_inputs = setup_inputs


def setup_inputs(seed=0):
    import zlib

    import numpy as np

    out = dict(_drawn_inputs(seed))
    spreads = {}
    factors = {}
    for name, (base, spread) in spreads.items():
        noise = np.random.default_rng([zlib.crc32(name.encode()), seed]).standard_normal(out[name].shape)
        drawn = base * np.exp(spread * noise) if base else spread * noise
        out[name] = jnp.asarray(drawn.astype(out[name].dtype))
    for name, factor in factors.items():
        out[name] = (out[name] * factor).astype(out[name].dtype)
    return out
```

```python
from contextlib import ExitStack

import concourse.bass as bass
from concourse import mybir


P = 128
ALPHA = 0.2
NEG = -9000000000000000.0
EPS = 1e-5

ALU = mybir.AluOpType
ACT = mybir.ActivationFunctionType
F32 = mybir.dt.float32
BF16 = mybir.dt.bfloat16
I32 = mybir.dt.int32
AX_X = mybir.AxisListType.X

D = 128
S2, S1 = D, D + 1
AUG = D + 2
ONE = D + 2
ROW = D + 4


def weights_stage(nc, const, W_dram, a_dram):
    L = len(W_dram)
    ident, waug = const["ident"], const["waug"]
    with ExitStack() as ctx:
        w_t = ctx.enter_context(nc.sbuf_tensor("w_t", [P, L, D], F32))
        a21 = ctx.enter_context(nc.sbuf_tensor("a21", [P, L, 2], F32))
        ps_t = ctx.enter_context(nc.psum_tensor("ps_wt", [P, L, D], F32))
        ps_a = ctx.enter_context(nc.psum_tensor("ps_wa", [P, L, 2], F32))
        loaded = ctx.enter_context(nc.semaphore("weights_loaded"))
        blank = ctx.enter_context(nc.semaphore("ident_blank"))
        drawn = ctx.enter_context(nc.semaphore("ident_drawn"))
        turned = ctx.enter_context(nc.semaphore("w_turned"))
        kept = ctx.enter_context(nc.semaphore("wt_kept"))
        scored = ctx.enter_context(nc.semaphore("wa_scored"))
        done = ctx.enter_context(nc.semaphore("waug_done"))
        block = ctx.enter_context(nc.Block())

        @block.sync
        def _(sp):
            for l in range(L):
                sp.dma_start(waug[:, l, 0:D], W_dram[l]).then_inc(loaded, 16)
                sp.dma_start(a21[:, l, 0:1], a_dram[l][D:2 * D, :]).then_inc(loaded, 16)
                sp.dma_start(a21[:, l, 1:2], a_dram[l][0:D, :]).then_inc(loaded, 16)

        @block.gpsimd
        def _(pool):
            nc.gpsimd.memset(ident[:], 0.0).then_inc(blank, 1)
            pool.wait_ge(blank, 1)
            nc.gpsimd.affine_select(out=ident[:], in_=ident[:], compare_op=ALU.not_equal, fill=1.0,
                                    base=0, pattern=[[-1, P]], channel_multiplier=1).then_inc(drawn, 1)

        @block.tensor
        def _(pe):
            pe.wait_ge(loaded, 48 * L)
            pe.wait_ge(drawn, 1)
            for l in range(L):
                nc.tensor.transpose(ps_t[:, l, :], waug[:, l, 0:D], ident[:]).then_inc(turned, 1)
            pe.wait_ge(kept, 1)
            for l in range(L):
                nc.tensor.matmul(ps_a[:, l, :], w_t[:, l, :], a21[:, l, :], start=True, stop=True).then_inc(scored, 1)

        @block.vector
        def _(dve):
            nc.vector.memset(const["eps"][:], EPS).then_inc(done, 1)
            dve.wait_ge(turned, L)
            nc.vector.tensor_copy(w_t[:], ps_t[:]).then_inc(kept, 1)
            dve.wait_ge(scored, L)
            nc.vector.tensor_copy(waug[:, :, S2:AUG], ps_a[:]).then_inc(done, 1)


def node_transform(nc, const, layer, x_dram, table, s2_line):
    N = x_dram.shape[0]
    Q = 4
    STEPS = N // (Q * P)
    x_v = x_dram.rearrange("(s q p) d -> s p q d", q=Q, p=P)
    t_v = table.rearrange("(s q p) d -> s p q d", q=Q, p=P)
    ident, waug, eps = const["ident"], const["waug"], const["eps"]
    with ExitStack() as ctx:
        def sb(name, shape):
            return ctx.enter_context(nc.sbuf_tensor(f"{name}{layer}", shape, F32))

        def sem(name):
            return ctx.enter_context(nc.semaphore(f"{name}{layer}"))

        x_in = sb("x_in", [P, 2, Q, D])
        stats = sb("stats", [P, 2, Q, 6])
        mv = sb("mv", [P, 2, Q, 2])
        std = sb("std", [P, 2, Q])
        rstd = sb("rstd", [P, 2, Q])
        h_t = sb("h_t", [P, 2, Q, P])
        rows = sb("rows", [P, 2, Q, ROW])
        ps_h = [ctx.enter_context(nc.psum_tensor(f"ps_h{b}_{layer}", [P, Q, P], F32)) for b in range(2)]
        ps_w = [ctx.enter_context(nc.psum_tensor(f"ps_w{b}_{layer}", [P, Q, 256], F32)) for b in range(2)]
        line = sb("line", [1, 2, Q * P])
        ps_l = [ctx.enter_context(nc.psum_tensor(f"ps_l{b}_{layer}", [1, Q * P], F32)) for b in range(2)]
        x_loaded = [sem(f"x_loaded{b}_") for b in range(2)]
        x_free = sem("x_free")
        stat = sem("stat")
        aggr = sem("aggr")
        rooted = sem("rooted")
        inverted = sem("inverted")
        normed = sem("normed")
        turned = sem("turned")
        relued = sem("relued")
        multiplied = sem("multiplied")
        row_ready = sem("row_ready")
        padded = sem("padded")
        stored = [sem(f"stored{b}_") for b in range(2)]
        block = ctx.enter_context(nc.Block())

        @block.sync
        def _(sp):
            with sp.Fori(0, STEPS // 2) as i:
                for b in range(2):
                    sp.wait_ge(x_free, 2 * i + b + 1)
                    sp.dma_start(x_in[:, b], x_v[bass.ds(2 * i + b, 1)].rearrange("o p q d -> (o p) q d")).then_inc(x_loaded[b], 16)

        @block.vector
        def _(dve):
            nc.vector.memset(rows[:], 1.0).then_inc(padded, 1)
            dve.sem_inc(x_free, 2)
            with dve.Fori(0, STEPS // 2) as i:
                for b in range(2):
                    s = 2 * i + b
                    dve.wait_ge(x_loaded[b], 16 * i + 16)
                    for q in range(Q):
                        nc.vector.bn_stats(stats[:, b, q, :], x_in[:, b, q, :]).then_inc(stat, 1)
                    dve.wait_ge(stat, Q * s + Q)
                    dve.nop(nofuse=True)
                    for q in range(Q):
                        nc.vector.bn_aggr(mv[:, b, q, :], stats[:, b, q, :]).then_inc(aggr, 1)
                    dve.wait_ge(rooted, s + 1)
                    nc.vector.reciprocal(rstd[:, b, :], std[:, b, :]).then_inc(inverted, 1)
                    dve.wait_ge(inverted, s + 1)
                    for q in range(Q):
                        op = nc.vector.tensor_scalar(x_in[:, b, q, :], x_in[:, b, q, :], mv[:, b, q, 0:1],
                                                     rstd[:, b, q:q + 1], ALU.subtract, ALU.mult)
                    op.then_inc(normed, 1)

        @block.scalar
        def _(act):
            act.wait_ge(padded, 1)
            for b in range(2):
                act.sem_inc(stored[b], 32)
            with act.Fori(0, STEPS // 2) as i:
                for b in range(2):
                    s = 2 * i + b
                    act.wait_ge(aggr, Q * s + Q)
                    nc.scalar.activation(std[:, b, :], mv[:, b, :, 1], ACT.Sqrt, bias=eps[:, 0:1]).then_inc(rooted, 1)
                    act.wait_ge(turned, s + 1)
                    nc.scalar.activation(h_t[:, b], ps_h[b][:], ACT.Relu).then_inc(relued, 1)
                    act.sem_inc(x_free, 1)
                    act.wait_ge(multiplied, s + 1)
                    act.wait_ge(stored[b], 32 * i + 32)
                    nc.scalar.activation(rows[:, b, :, 0:AUG], ps_w[b][:, :, 0:AUG], ACT.Copy).then_inc(row_ready, 1)
                    nc.scalar.activation(line[:, b], ps_l[b][:], ACT.Copy).then_inc(row_ready, 1)
                    act.wait_ge(row_ready, 2 * s + 2)
                    act.dma_start(t_v[bass.ds(s, 1)].rearrange("o p q d -> (o p) q d"), rows[:, b]).then_inc(stored[b], 16)
                    act.dma_start(s2_line[:, bass.ds(s * (Q * P), Q * P)], line[:, b]).then_inc(stored[b], 16)
            for b in range(2):
                act.wait_ge(stored[b], 32 * (STEPS // 2 + 1))

        @block.tensor
        def _(pe):
            with pe.Fori(0, STEPS // 2) as i:
                for b in range(2):
                    s = 2 * i + b
                    pe.wait_ge(normed, s + 1)
                    for q in range(Q):
                        op = nc.tensor.transpose(ps_h[b][:, q, :], x_in[:, b, q, :], ident[:])
                    op.then_inc(turned, 1)
                    pe.wait_ge(relued, s + 1)
                    for q in range(Q):
                        op = nc.tensor.matmul(ps_w[b][:, q, 0:AUG], h_t[:, b, q, :], waug[:, layer, :], start=True, stop=True)
                    op = nc.tensor.matmul(ps_l[b][:], waug[:, layer, S2:S2 + 1], h_t[:, b].rearrange("p q n -> p (q n)"),
                                          start=True, stop=True)
                    op.then_inc(multiplied, 1)


def dense_attention(nc, const, layer, table, s2_line, adj, x_dram, dst):
    N = x_dram.shape[0]
    NB = N // P
    CW = 2048
    NCH = N // CW
    EW = 512
    NE = N // EW
    KQ = EW // P
    BIG = -2.0 * NEG
    ident = const["ident"]
    x_v = x_dram.rearrange("(t p) d -> t p d", p=P)
    dst_v = dst.rearrange("(t p) d -> t p d", p=P)
    adj_v = adj.rearrange("(t p) (c w) -> t c p w", p=P, w=CW)
    t_v = table.rearrange("(t p) d -> p t d", p=P)
    with ExitStack() as ctx:
        def sb(name, shape, dt=F32):
            return ctx.enter_context(nc.sbuf_tensor(f"{name}{layer}", shape, dt))

        def sem(name):
            return ctx.enter_context(nc.semaphore(f"{name}{layer}"))

        wh = sb("d_wh", [P, NB, ROW])
        s2b = sb("d_s2b", [P, N])
        adj_in = sb("d_adj", [P, NCH, CW], I32)
        pen = sb("d_pen", [P, CW])
        e = sb("d_e", [P, N])
        mx = sb("d_mx", [P, NCH])
        neg_max = sb("d_negmax", [P, 1])
        p_row = sb("d_p", [P, 2, EW])
        p_t = sb("d_pt", [P, 2, KQ, P])
        x_in = sb("d_x", [P, D])
        rden = sb("d_rden", [P, 1])
        o = sb("d_o", [P, D])
        low = sb("d_low", [P, D])
        ex = sb("d_ex", [P, D])
        res = sb("d_res", [P, D])
        fin = sb("d_fin", [P, D])
        ps_t = [ctx.enter_context(nc.psum_tensor(f"d_pst{b}_{layer}", [P, KQ, P], F32)) for b in range(2)]
        ps_o = ctx.enter_context(nc.psum_tensor(f"d_pso_{layer}", [P, ONE + 1], F32))
        resident = sem("d_resident")
        adj_loaded = [sem(f"d_adj_loaded{c}_") for c in range(NCH)]
        adj_free = sem("d_adj_free")
        x_loaded = sem("d_x_loaded")
        x_free = sem("d_x_free")
        step = sem("d_step")
        maxed = sem("d_maxed")
        exped = sem("d_exped")
        e_free = sem("d_e_free")
        turned = sem("d_turned")
        kept = sem("d_kept")
        summed = sem("d_summed")
        o_step = sem("d_o_step")
        low_ready = sem("d_low_ready")
        ex_ready = sem("d_ex_ready")
        fin_ready = sem("d_fin_ready")
        stored = sem("d_stored")
        block = ctx.enter_context(nc.Block())
        C_STEP = 4 * NCH

        @block.sync
        def _(sp):
            sp.dma_start(wh[:], t_v).then_inc(resident, 16)
            sp.dma_start(s2b[:], s2_line.to_broadcast([P, N])).then_inc(resident, 16)
            with sp.Fori(0, NB) as t:
                for c in range(NCH):
                    sp.wait_ge(adj_free, NCH * t + c + 1)
                    sp.dma_start(adj_in[:, c, :], adj_v[bass.ds(t, 1), c].rearrange("o p w -> (o p) w")).then_inc(adj_loaded[c], 16)
                sp.wait_ge(x_free, t + 1)
                sp.dma_start(x_in[:], x_v[bass.ds(t, 1)].rearrange("o p d -> (o p) d")).then_inc(x_loaded, 16)
                sp.wait_ge(fin_ready, t + 1)
                sp.dma_start(dst_v[bass.ds(t, 1)].rearrange("o p d -> (o p) d"), fin[:]).then_inc(stored, 16)
            sp.wait_ge(stored, 16 * NB + 16)

        @block.vector
        def _(dve):
            dve.sem_inc(adj_free, NCH)
            dve.sem_inc(x_free, 1)
            dve.sem_inc(stored, 16)
            dve.wait_ge(resident, 32)
            with dve.Fori(0, NB) as t:
                dve.wait_ge(e_free, t + 1)
                for c in range(NCH):
                    ec = e[:, c * CW:(c + 1) * CW]
                    nc.vector.tensor_scalar(ec, s2b[:, c * CW:(c + 1) * CW], wh[:, bass.ds(t, 1), S1], None, ALU.add).then_inc(step, 1)
                    dve.wait_ge(step, C_STEP * t + 4 * c + 1)
                    nc.vector.scalar_tensor_tensor(ec, ec, ALPHA, ec, ALU.mult, ALU.max).then_inc(step, 1)
                    dve.wait_ge(adj_loaded[c], 16 * t + 16)
                    nc.vector.tensor_scalar(pen[:], adj_in[:, c, :], 0, BIG, ALU.is_gt, ALU.mult).then_inc(step, 1)
                    dve.wait_ge(step, C_STEP * t + 4 * c + 3)
                    dve.sem_inc(adj_free, 1)
                    nc.vector.scalar_tensor_tensor(ec, pen[:], NEG, ec, ALU.add, ALU.min).then_inc(step, 1)
                    dve.wait_ge(step, C_STEP * t + 4 * c + 4)
                    op = nc.vector.reduce_max(mx[:, c:c + 1], ec, AX_X)
                    op.then_inc(maxed, 1)
                dve.wait_ge(maxed, (NCH + 1) * t + NCH)
                nc.vector.tensor_reduce(neg_max[:], mx[:], AX_X, ALU.max, negate=True).then_inc(maxed, 1)
                for c in range(NE):
                    dve.wait_ge(turned, NE * t + c + 1)
                    nc.vector.tensor_copy(p_t[:, c % 2], ps_t[c % 2][:]).then_inc(kept, 1)
                dve.wait_ge(summed, t + 1)
                nc.vector.reciprocal(rden[:], ps_o[:, ONE:ONE + 1]).then_inc(o_step, 1)
                dve.wait_ge(o_step, 2 * t + 1)
                nc.vector.tensor_scalar(o[:], ps_o[:, 0:D], rden[:, 0:1], None, ALU.mult).then_inc(o_step, 1)
                dve.wait_ge(o_step, 2 * t + 2)
                nc.vector.tensor_scalar(low[:], o[:], 0.0, None, ALU.min).then_inc(low_ready, 1)
                dve.wait_ge(x_loaded, 16 * t + 16)
                nc.vector.scalar_tensor_tensor(res[:], o[:], 0.0, x_in[:], ALU.max, ALU.add).then_inc(x_free, 1)
                dve.wait_ge(x_free, t + 2)
                dve.wait_ge(ex_ready, t + 1)
                dve.wait_ge(stored, 16 * t + 16)
                nc.vector.scalar_tensor_tensor(fin[:], ex[:], -1.0, res[:], ALU.add, ALU.add).then_inc(fin_ready, 1)

        @block.scalar
        def _(act):
            act.sem_inc(e_free, 1)
            with act.Fori(0, NB) as t:
                act.wait_ge(maxed, (NCH + 1) * t + NCH + 1)
                for c in range(NE):
                    act.wait_ge(turned, NE * t + c + 1 - 2) if c >= 2 else None
                    nc.scalar.activation(p_row[:, c % 2, :], e[:, c * EW:(c + 1) * EW], ACT.Exp,
                                         bias=neg_max[:, 0:1]).then_inc(exped, 1)
                act.wait_ge(exped, NE * t + NE)
                act.sem_inc(e_free, 1)
                act.wait_ge(low_ready, t + 1)
                nc.scalar.activation(ex[:], low[:], ACT.Exp).then_inc(ex_ready, 1)

        @block.tensor
        def _(pe):
            pe.wait_ge(resident, 32)

            def product(t, c):
                pe.wait_ge(kept, NE * t + c + 1)
                for q in range(KQ):
                    op = nc.tensor.matmul(ps_o[:], p_t[:, c % 2, q, :], wh[:, KQ * c + q, 0:ONE + 1],
                                          start=(c == 0 and q == 0), stop=(c == NE - 1 and q == KQ - 1))
                if c == NE - 1:
                    op.then_inc(summed, 1)

            with pe.Fori(0, NB) as t:
                for c in range(NE):
                    pe.wait_ge(exped, NE * t + c + 1)
                    for q in range(KQ):
                        op = nc.tensor.transpose(ps_t[c % 2][:, q, :], p_row[:, c % 2, q * P:(q + 1) * P], ident[:])
                    op.then_inc(turned, 1)
                    if c >= 1:
                        product(t, c - 1)
                product(t, NE - 1)


def gat_kernel(nc, x, adj, W0, a0, W1, a1, out):
    N = x.shape[0]
    table = [nc.dram_tensor(f"table{l}", [N, ROW], F32, kind="Internal").ap() for l in range(2)]
    s2_line = [nc.dram_tensor(f"s2_line{l}", [1, N], F32, kind="Internal").ap() for l in range(2)]
    x_mid = nc.dram_tensor("x_mid", [N, D], F32, kind="Internal").ap()
    with ExitStack() as ctx:
        def sb(name, shape, dt=F32):
            return ctx.enter_context(nc.sbuf_tensor(name, shape, dt))

        const = {
            "ident": sb("ident", [P, P]),
            "waug": sb("waug", [P, 2, AUG]),
            "eps": sb("eps", [P, 1]),
        }
        weights_stage(nc, const, [W0, W1], [a0, a1])
        node_transform(nc, const, 0, x, table[0], s2_line[0])
        dense_attention(nc, const, 0, table[0], s2_line[0], adj, x, x_mid)
        node_transform(nc, const, 1, x_mid, table[1], s2_line[1])
        dense_attention(nc, const, 1, table[1], s2_line[1], adj, x_mid, out)


_INS = ["x", "adj", "L0_gnn_W", "L0_gnn_a", "L1_gnn_W", "L1_gnn_a"]


def kernel(**inputs):
    import numpy as _np
    import concourse.bacc as _bacc
    from concourse import mybir as _mybir
    from concourse.bass_utils import run_bass_kernel_spmd as _run

    nc = _bacc.Bacc("TRN2", target_bir_lowering=False, num_devices=1)
    arrays, args = {}, []
    for name in _INS:
        a = _np.ascontiguousarray(inputs[name])
        arrays[f"in_{name}"] = a
        args.append(nc.dram_tensor(f"in_{name}", a.shape, _mybir.dt.from_np(a.dtype), kind="ExternalInput").ap())
    out = nc.dram_tensor("out", inputs["x"].shape, _mybir.dt.float32, kind="ExternalOutput").ap()
    gat_kernel(nc, *args, out)
    r = _run(nc, [arrays], core_ids=[0])
    return r.results[0]["out"]
```

```python
from contextlib import ExitStack, contextmanager

import concourse.bass as bass
from concourse import mybir


P = 128
ALPHA = 0.2
NEG = -9000000000000000.0
EPS = 1e-5

ALU = mybir.AluOpType
ACT = mybir.ActivationFunctionType
F32 = mybir.dt.float32
BF16 = mybir.dt.bfloat16
I32 = mybir.dt.int32
U32 = mybir.dt.uint32
AX_X = mybir.AxisListType.X

D = 128
S2, S1 = D, D + 1
AUG = D + 2
ONE = D + 2
ROW = D + 4

CAND = 8
SLOTS = 32
DEG, OWN = SLOTS, SLOTS + 1
REC = SLOTS + 4
LOW = 256


def weights_stage(nc, const, W_dram, a_dram):
    L = len(W_dram)
    ident, waug = const["ident"], const["waug"]
    with ExitStack() as ctx:
        w_t = ctx.enter_context(nc.sbuf_tensor("w_t", [P, L, D], F32))
        a21 = ctx.enter_context(nc.sbuf_tensor("a21", [P, L, 2], F32))
        ps_t = ctx.enter_context(nc.psum_tensor("ps_wt", [P, L, D], F32))
        ps_a = ctx.enter_context(nc.psum_tensor("ps_wa", [P, L, 2], F32))
        loaded = signal(nc, const, "weights_loaded")
        blank = signal(nc, const, "ident_blank")
        drawn = signal(nc, const, "ident_drawn")
        turned = signal(nc, const, "w_turned")
        kept = signal(nc, const, "wt_kept")
        scored = signal(nc, const, "wa_scored")
        done = signal(nc, const, "waug_done")
        block = ctx.enter_context(nc.Block())

        @block.sync
        def _(sp):
            for l in range(L):
                sp.dma_start(waug[:, l, 0:D], W_dram[l]).then_inc(loaded, 16)
                sp.dma_start(a21[:, l, 0:1], a_dram[l][D:2 * D, :]).then_inc(loaded, 16)
                sp.dma_start(a21[:, l, 1:2], a_dram[l][0:D, :]).then_inc(loaded, 16)

        @block.gpsimd
        def _(pool):
            nc.gpsimd.memset(ident[:], 0.0).then_inc(blank, 1)
            pool.wait_ge(blank, 1)
            nc.gpsimd.affine_select(out=ident[:], in_=ident[:], compare_op=ALU.not_equal, fill=1.0,
                                    base=0, pattern=[[-1, P]], channel_multiplier=1).then_inc(drawn, 1)

        @block.tensor
        def _(pe):
            pe.wait_ge(loaded, 48 * L)
            pe.wait_ge(drawn, 1)
            for l in range(L):
                nc.tensor.transpose(ps_t[:, l, :], waug[:, l, 0:D], ident[:]).then_inc(turned, 1)
            pe.wait_ge(kept, 1)
            for l in range(L):
                nc.tensor.matmul(ps_a[:, l, :], w_t[:, l, :], a21[:, l, :], start=True, stop=True).then_inc(scored, 1)

        @block.vector
        def _(dve):
            nc.vector.memset(const["eps"][:], EPS).then_inc(done, 1)
            dve.wait_ge(turned, L)
            nc.vector.tensor_copy(w_t[:], ps_t[:]).then_inc(kept, 1)
            dve.wait_ge(scored, L)
            nc.vector.tensor_copy(waug[:, :, S2:AUG], ps_a[:]).then_inc(done, 1)


def signal(nc, const, name):
    const["signals"].append(nc.alloc_semaphore(name))
    return const["signals"][-1]


@contextmanager
def when(engine, flag):
    if flag is None:
        yield
    else:
        with engine.If(engine.value_load(flag[0:1, 0:1], min_val=0, max_val=P) > 0):
            yield


def node_transform(nc, const, layer, x_dram, table, self_rows, s2_line, only_if=None):
    N = x_dram.shape[0]
    tag = "" if only_if is None else "again"
    Q = 4
    STEPS = N // (Q * P)
    x_v = x_dram.rearrange("(s q p) d -> s p q d", q=Q, p=P)
    t_v = table.rearrange("(s q p) d -> s p q d", q=Q, p=P)
    self_v = self_rows.rearrange("(s q p) d -> s p q d", q=Q, p=P)
    mean_wh = const["mean_wh"]
    ident, waug, eps = const["ident"], const["waug"], const["eps"]
    with ExitStack() as ctx:
        def sb(name, shape):
            return ctx.enter_context(nc.sbuf_tensor(f"{name}{tag}{layer}", shape, F32))

        def sem(name):
            return signal(nc, const, f"{name}{tag}{layer}")

        x_in = sb("x_in", [P, 2, Q, ROW])
        x_hat = sb("x_hat", [P, 2, Q, D])
        h_sums = sb("h_sums", [P, STEPS])
        h_sum = sb("h_sum", [P, 1])
        h_sum_wide = sb("h_sum_wide", [P, P])
        stats = sb("stats", [P, 2, Q, 6])
        mv = sb("mv", [P, 2, Q, 2])
        std = sb("std", [P, 2, Q])
        rstd = sb("rstd", [P, 2, Q])
        h_t = sb("h_t", [P, 2, Q, P])
        rows = sb("rows", [P, 2, Q, ROW])
        ps_h = [ctx.enter_context(nc.psum_tensor(f"ps_h{b}_{tag}{layer}", [P, Q, P], F32)) for b in range(2)]
        ps_w = [ctx.enter_context(nc.psum_tensor(f"ps_w{b}_{tag}{layer}", [P, Q, 256], F32)) for b in range(2)]
        summed = sem("h_summed")
        widened = sem("h_widened")
        averaged = sem("averaged")
        mean_ready = sem("mean_ready")
        line = sb("line", [1, 2, Q * P])
        ps_l = [ctx.enter_context(nc.psum_tensor(f"ps_l{b}_{tag}{layer}", [P, Q * P], F32)) for b in range(2)]
        x_loaded = [sem(f"x_loaded{b}_") for b in range(2)]
        x_padded = sem("x_padded")
        warm = sb("warm", [P, 1])
        warmed = sem("warmed")
        x_hat_free = sem("x_hat_free")
        stat = sem("stat")
        aggr = sem("aggr")
        rooted = sem("rooted")
        inverted = sem("inverted")
        normed = sem("normed")
        turned = sem("turned")
        relued = sem("relued")
        multiplied = sem("multiplied")
        row_ready = sem("row_ready")
        padded = sem("padded")
        stored = [sem(f"stored{b}_") for b in range(2)]
        block = ctx.enter_context(nc.Block())

        @block.sync
        def _(sp):
            with when(sp, only_if):
                with sp.Fori(0, STEPS // 2) as i:
                    for b in range(2):
                        sp.wait_ge(x_padded, 1)
                        sp.wait_ge(stored[b], 48 * i + 48)
                        sp.dma_start(x_in[:, b, :, 0:D], x_v[bass.ds(2 * i + b, 1)].rearrange("o p q d -> (o p) q d")).then_inc(x_loaded[b], 16)

        @block.vector
        def _(dve):
            with when(dve, only_if):
                nc.vector.memset(rows[:], 1.0).then_inc(padded, 1)
                nc.vector.memset(x_in[:, :, :, D:ROW], 0.0).then_inc(padded, 1)
                dve.wait_ge(padded, 2)
                dve.sem_inc(x_padded, 1)
                with dve.Fori(0, STEPS // 2) as i:
                    for b in range(2):
                        s = 2 * i + b
                        dve.wait_ge(x_loaded[b], 16 * i + 16)
                        for q in range(Q):
                            nc.vector.bn_stats(stats[:, b, q, :], x_in[:, b, q, 0:D]).then_inc(stat, 1)
                        dve.wait_ge(stat, Q * s + Q)
                        dve.nop(nofuse=True)
                        for q in range(Q):
                            nc.vector.bn_aggr(mv[:, b, q, :], stats[:, b, q, :]).then_inc(aggr, 1)
                        dve.wait_ge(rooted, s + 1)
                        nc.vector.reciprocal(rstd[:, b, :], std[:, b, :]).then_inc(inverted, 1)
                        dve.wait_ge(inverted, s + 1)
                        dve.wait_ge(x_hat_free, s + 1)
                        for q in range(Q):
                            op = nc.vector.tensor_scalar(x_hat[:, b, q, :], x_in[:, b, q, 0:D], mv[:, b, q, 0:1],
                                                         rstd[:, b, q:q + 1], ALU.subtract, ALU.mult)
                        op.then_inc(normed, 1)
                dve.wait_ge(relued, STEPS)
                nc.vector.reduce_sum(h_sum[:], h_sums[:], AX_X).then_inc(summed, 1)
                dve.wait_ge(summed, 1)
                nc.vector.tensor_copy(h_sum_wide[:], h_sum[:].to_broadcast([P, P])).then_inc(widened, 1)
                dve.wait_ge(averaged, 1)
                nc.vector.tensor_scalar(mean_wh[:], ps_l[0][:, 0:D], 1.0 / N, None, ALU.mult).then_inc(mean_ready, 1)

        @block.scalar
        def _(act):
            with when(act, only_if):
                act.wait_ge(padded, 2)
                act.sem_inc(x_hat_free, 2)
                nc.scalar.activation(warm[:], eps[:], ACT.Sqrt).then_inc(warmed, 1)
                for b in range(2):
                    act.sem_inc(stored[b], 48)
                with act.Fori(0, STEPS // 2) as i:
                    for b in range(2):
                        s = 2 * i + b
                        act.wait_ge(aggr, Q * s + Q)
                        nc.scalar.activation(std[:, b, :], mv[:, b, :, 1], ACT.Sqrt, bias=eps[:, 0:1]).then_inc(rooted, 1)
                        act.wait_ge(turned, s + 1)
                        nc.scalar.activation(h_t[:, b], ps_h[b][:], ACT.Relu,
                                             accum_out=h_sums[:, bass.ds(s, 1)]).then_inc(relued, 1)
                        act.sem_inc(x_hat_free, 1)
                        act.wait_ge(multiplied, s + 1)
                        act.wait_ge(stored[b], 48 * i + 48)
                        nc.scalar.activation(rows[:, b, :, 0:AUG], ps_w[b][:, :, 0:AUG], ACT.Copy).then_inc(row_ready, 1)
                        nc.scalar.activation(x_in[:, b, :, D:D + 1], ps_w[b][:, :, S1:S1 + 1], ACT.Copy).then_inc(row_ready, 1)
                        nc.scalar.activation(line[:, b], ps_l[b][0:1, :], ACT.Copy).then_inc(row_ready, 1)
                        act.wait_ge(row_ready, 3 * s + 3)
                        act.dma_start(t_v[bass.ds(s, 1)].rearrange("o p q d -> (o p) q d"), rows[:, b]).then_inc(stored[b], 16)
                        act.dma_start(self_v[bass.ds(s, 1)].rearrange("o p q d -> (o p) q d"), x_in[:, b]).then_inc(stored[b], 16)
                        act.dma_start(s2_line[:, bass.ds(s * (Q * P), Q * P)], line[:, b]).then_inc(stored[b], 16)
                for b in range(2):
                    act.wait_ge(stored[b], 48 * (STEPS // 2 + 1))

        @block.tensor
        def _(pe):
            with when(pe, only_if):
                with pe.Fori(0, STEPS // 2) as i:
                    for b in range(2):
                        s = 2 * i + b
                        pe.wait_ge(normed, s + 1)
                        for q in range(Q):
                            op = nc.tensor.transpose(ps_h[b][:, q, :], x_hat[:, b, q, :], ident[:])
                        op.then_inc(turned, 1)
                        pe.wait_ge(relued, s + 1)
                        for q in range(Q):
                            op = nc.tensor.matmul(ps_w[b][:, q, 0:AUG], h_t[:, b, q, :], waug[:, layer, :], start=True, stop=True)
                        op = nc.tensor.matmul(ps_l[b][0:1, :], waug[:, layer, S2:S2 + 1], h_t[:, b].rearrange("p q n -> p (q n)"),
                                              start=True, stop=True)
                        op.then_inc(multiplied, 1)
                pe.wait_ge(widened, 1)
                pe.wait_ge(row_ready, 3 * STEPS)
                nc.tensor.matmul(ps_l[0][:, 0:D], h_sum_wide[:], waug[:, layer, 0:D], start=True, stop=True).then_inc(averaged, 1)


def dense_attention(nc, const, layer, table, s2_line, adj, x_dram, dst, only_if=None):
    N = x_dram.shape[0]
    NB = N // P
    CW = 2048
    NCH = N // CW
    EW = 512
    NE = N // EW
    KQ = EW // P
    BIG = -2.0 * NEG
    ident = const["ident"]
    x_v = x_dram.rearrange("(t p) d -> t p d", p=P)
    dst_v = dst.rearrange("(t p) d -> t p d", p=P)
    adj_v = adj.rearrange("(t p) (c w) -> t c p w", p=P, w=CW)
    t_v = table.rearrange("(t p) d -> p t d", p=P)
    with ExitStack() as ctx:
        def sb(name, shape, dt=F32):
            return ctx.enter_context(nc.sbuf_tensor(f"{name}{layer}", shape, dt))

        def sem(name):
            return signal(nc, const, f"{name}{layer}")

        wh = sb("d_wh", [P, NB, ROW])
        s2b = sb("d_s2b", [P, N])
        adj_in = sb("d_adj", [P, NCH, CW], I32)
        pen = sb("d_pen", [P, CW])
        e = sb("d_e", [P, N])
        mx = sb("d_mx", [P, NCH])
        neg_max = sb("d_negmax", [P, 1])
        p_row = sb("d_p", [P, 2, EW])
        p_t = sb("d_pt", [P, 2, KQ, P])
        x_in = sb("d_x", [P, D])
        rden = sb("d_rden", [P, 1])
        o = sb("d_o", [P, D])
        low = sb("d_low", [P, D])
        ex = sb("d_ex", [P, D])
        res = sb("d_res", [P, D])
        fin = sb("d_fin", [P, D])
        ps_t = [ctx.enter_context(nc.psum_tensor(f"d_pst{b}_{layer}", [P, KQ, P], F32)) for b in range(2)]
        ps_o = ctx.enter_context(nc.psum_tensor(f"d_pso_{layer}", [P, ONE + 1], F32))
        resident = sem("d_resident")
        adj_loaded = [sem(f"d_adj_loaded{c}_") for c in range(NCH)]
        adj_free = sem("d_adj_free")
        x_loaded = sem("d_x_loaded")
        x_free = sem("d_x_free")
        step = sem("d_step")
        maxed = sem("d_maxed")
        exped = sem("d_exped")
        e_free = sem("d_e_free")
        turned = sem("d_turned")
        kept = sem("d_kept")
        summed = sem("d_summed")
        o_step = sem("d_o_step")
        low_ready = sem("d_low_ready")
        ex_ready = sem("d_ex_ready")
        fin_ready = sem("d_fin_ready")
        stored = sem("d_stored")
        block = ctx.enter_context(nc.Block())
        C_STEP = 4 * NCH

        @block.sync
        def _(sp):
            with when(sp, only_if):
                sp.dma_start(wh[:], t_v).then_inc(resident, 16)
                sp.dma_start(s2b[:], s2_line.to_broadcast([P, N])).then_inc(resident, 16)
                with sp.Fori(0, NB) as t:
                    for c in range(NCH):
                        sp.wait_ge(adj_free, NCH * t + c + 1)
                        sp.dma_start(adj_in[:, c, :], adj_v[bass.ds(t, 1), c].rearrange("o p w -> (o p) w")).then_inc(adj_loaded[c], 16)
                    sp.wait_ge(x_free, t + 1)
                    sp.dma_start(x_in[:], x_v[bass.ds(t, 1)].rearrange("o p d -> (o p) d")).then_inc(x_loaded, 16)
                    sp.wait_ge(fin_ready, t + 1)
                    sp.dma_start(dst_v[bass.ds(t, 1)].rearrange("o p d -> (o p) d"), fin[:]).then_inc(stored, 16)
                sp.wait_ge(stored, 16 * NB + 16)

        @block.vector
        def _(dve):
            with when(dve, only_if):
                dve.sem_inc(adj_free, NCH)
                dve.sem_inc(x_free, 1)
                dve.sem_inc(stored, 16)
                dve.wait_ge(resident, 32)
                with dve.Fori(0, NB) as t:
                    dve.wait_ge(e_free, t + 1)
                    for c in range(NCH):
                        ec = e[:, c * CW:(c + 1) * CW]
                        nc.vector.tensor_scalar(ec, s2b[:, c * CW:(c + 1) * CW], wh[:, bass.ds(t, 1), S1], None, ALU.add).then_inc(step, 1)
                        dve.wait_ge(step, C_STEP * t + 4 * c + 1)
                        nc.vector.scalar_tensor_tensor(ec, ec, ALPHA, ec, ALU.mult, ALU.max).then_inc(step, 1)
                        dve.wait_ge(adj_loaded[c], 16 * t + 16)
                        nc.vector.tensor_scalar(pen[:], adj_in[:, c, :], 0, BIG, ALU.is_gt, ALU.mult).then_inc(step, 1)
                        dve.wait_ge(step, C_STEP * t + 4 * c + 3)
                        dve.sem_inc(adj_free, 1)
                        nc.vector.scalar_tensor_tensor(ec, pen[:], NEG, ec, ALU.add, ALU.min).then_inc(step, 1)
                        dve.wait_ge(step, C_STEP * t + 4 * c + 4)
                        op = nc.vector.reduce_max(mx[:, c:c + 1], ec, AX_X)
                        op.then_inc(maxed, 1)
                    dve.wait_ge(maxed, (NCH + 1) * t + NCH)
                    nc.vector.tensor_reduce(neg_max[:], mx[:], AX_X, ALU.max, negate=True).then_inc(maxed, 1)
                    for c in range(NE):
                        dve.wait_ge(turned, NE * t + c + 1)
                        nc.vector.tensor_copy(p_t[:, c % 2], ps_t[c % 2][:]).then_inc(kept, 1)
                    dve.wait_ge(summed, t + 1)
                    nc.vector.reciprocal(rden[:], ps_o[:, ONE:ONE + 1]).then_inc(o_step, 1)
                    dve.wait_ge(o_step, 2 * t + 1)
                    nc.vector.tensor_scalar(o[:], ps_o[:, 0:D], rden[:, 0:1], None, ALU.mult).then_inc(o_step, 1)
                    dve.wait_ge(o_step, 2 * t + 2)
                    nc.vector.tensor_scalar(low[:], o[:], 0.0, None, ALU.min).then_inc(low_ready, 1)
                    dve.wait_ge(x_loaded, 16 * t + 16)
                    nc.vector.scalar_tensor_tensor(res[:], o[:], 0.0, x_in[:], ALU.max, ALU.add).then_inc(x_free, 1)
                    dve.wait_ge(x_free, t + 2)
                    dve.wait_ge(ex_ready, t + 1)
                    dve.wait_ge(stored, 16 * t + 16)
                    nc.vector.scalar_tensor_tensor(fin[:], ex[:], -1.0, res[:], ALU.add, ALU.add).then_inc(fin_ready, 1)

        @block.scalar
        def _(act):
            with when(act, only_if):
                act.sem_inc(e_free, 1)
                with act.Fori(0, NB) as t:
                    act.wait_ge(maxed, (NCH + 1) * t + NCH + 1)
                    for c in range(NE):
                        act.wait_ge(turned, NE * t + c + 1 - 2) if c >= 2 else None
                        nc.scalar.activation(p_row[:, c % 2, :], e[:, c * EW:(c + 1) * EW], ACT.Exp,
                                             bias=neg_max[:, 0:1]).then_inc(exped, 1)
                    act.wait_ge(exped, NE * t + NE)
                    act.sem_inc(e_free, 1)
                    act.wait_ge(low_ready, t + 1)
                    nc.scalar.activation(ex[:], low[:], ACT.Exp).then_inc(ex_ready, 1)

        @block.tensor
        def _(pe):
            with when(pe, only_if):
                pe.wait_ge(resident, 32)

                def product(t, c):
                    pe.wait_ge(kept, NE * t + c + 1)
                    for q in range(KQ):
                        op = nc.tensor.matmul(ps_o[:], p_t[:, c % 2, q, :], wh[:, KQ * c + q, 0:ONE + 1],
                                              start=(c == 0 and q == 0), stop=(c == NE - 1 and q == KQ - 1))
                    if c == NE - 1:
                        op.then_inc(summed, 1)

                with pe.Fori(0, NB) as t:
                    for c in range(NE):
                        pe.wait_ge(exped, NE * t + c + 1)
                        for q in range(KQ):
                            op = nc.tensor.transpose(ps_t[c % 2][:, q, :], p_row[:, c % 2, q * P:(q + 1) * P], ident[:])
                        op.then_inc(turned, 1)
                        if c >= 1:
                            product(t, c - 1)
                    product(t, NE - 1)


def scan_edges(nc, const, adj, keys, crowded):
    N = adj.shape[0]
    NT = N // P
    CW = 2048
    NCH = N // CW
    BW = 512
    NB = CW // BW
    adj_v = adj.rearrange("(t p) (c w) -> t c p w", p=P, w=CW)
    with ExitStack() as ctx:
        def sb(name, shape, dt=F32):
            return ctx.enter_context(nc.sbuf_tensor(name, shape, dt))

        def sem(name):
            return signal(nc, const, name)

        adj_in = sb("s_adj", [P, NCH, CW], I32)
        edge = sb("s_edge", [P, NCH, CW], BF16)
        lift = sb("s_lift", [P, P], BF16)
        ones2 = sb("s_ones2", [2, P], BF16)
        col = sb("s_col", [2, N], BF16)
        col_high = sb("s_col_high", [1, N], BF16)
        cand = sb("s_cand", [P, 2, N // BW, CAND])
        rest = sb("s_rest", [P, 2, N // BW * CAND])
        top = sb("s_top", [P, SLOTS])
        ps = [ctx.enter_context(nc.psum_tensor(f"s_ps{b}", [P, NB, BW], F32)) for b in range(2)]
        adj_loaded = [sem(f"s_adj_loaded{c}") for c in range(NCH)]
        edge_ready = sem("s_edge_ready")
        lifted = sem("s_lifted")
        numbered = sem("s_numbered")
        col_ready = sem("s_col_ready")
        keyed = sem("s_keyed")
        picked = sem("s_picked")
        listed = sem("s_listed")
        blank = sem("s_blank")
        KEYED0, PICKED0, EDGE0, LISTED0 = NCH, 2, NCH, 1
        block = ctx.enter_context(nc.Block())

        @block.sync
        def _(sp):
            sp.wait_ge(numbered, 2)
            sp.dma_start(col[1:2, :], col_high[:]).then_inc(col_ready, 16)
            with sp.Fori(0, NT) as t:
                for c in range(NCH):
                    sp.wait_ge(edge_ready, NCH * t + c + 1)
                    sp.dma_start(adj_in[:, c, :], adj_v[bass.ds(t, 1), c].rearrange("o p w -> (o p) w")).then_inc(adj_loaded[c], 16)

        @block.gpsimd
        def _(pool):
            nc.gpsimd.memset(lift[:], 0.0).then_inc(lifted, 1)
            pool.wait_ge(lifted, 1)
            nc.gpsimd.affine_select(out=lift[:], in_=lift[:], compare_op=ALU.not_equal, fill=float(N),
                                    base=0, pattern=[[-1, P]], channel_multiplier=1).then_inc(lifted, 1)
            nc.gpsimd.memset(ones2[:], 1.0).then_inc(lifted, 1)
            nc.gpsimd.iota(col[0:1, :], [[0, N // LOW], [1, LOW]], base=0, channel_multiplier=0,
                           allow_small_or_imprecise_dtypes=True).then_inc(numbered, 1)
            nc.gpsimd.iota(col_high[:], [[LOW, N // LOW], [0, LOW]], base=0, channel_multiplier=0,
                           allow_small_or_imprecise_dtypes=True).then_inc(numbered, 1)

        @block.scalar
        def _(act):
            act.sem_inc(edge_ready, EDGE0)
            with act.Fori(0, NT) as t:
                for c in range(NCH):
                    act.wait_ge(adj_loaded[c], 16 * t + 16)
                    act.wait_ge(keyed, NCH * t + c + 1)
                    nc.scalar.activation(edge[:, c, :], adj_in[:, c, :], ACT.Sign).then_inc(edge_ready, 1)

        @block.tensor
        def _(pe):
            pe.sem_inc(keyed, KEYED0)
            pe.wait_ge(lifted, 3)
            pe.wait_ge(col_ready, 16)
            with pe.Fori(0, NT) as t:
                for c in range(NCH):
                    pe.wait_ge(picked, NCH * t + c + 1)
                    for w in range(NB):
                        nc.tensor.matmul(ps[c % 2][:, w, :], ones2[:], col[:, (c * NB + w) * BW:(c * NB + w + 1) * BW],
                                         start=True, stop=False)
                    pe.wait_ge(edge_ready, EDGE0 + NCH * t + c + 1)
                    for w in range(NB):
                        op = nc.tensor.matmul(ps[c % 2][:, w, :], lift[:], edge[:, c, w * BW:(w + 1) * BW],
                                              start=False, stop=True)
                    op.then_inc(keyed, 1)

        @block.vector
        def _(dve):
            ROUNDS = SLOTS // CAND
            OPS = 2 * ROUNDS + 1

            def settled(value):
                dve.wait_ge(listed, value)
                dve.nop(nofuse=True)

            def listing(n, t, b):
                at = LISTED0 + OPS * t + n
                flat = cand[:, b].rearrange("p b k -> p (b k)")
                m = n - 1
                if n == 0:
                    dve.wait_ge(picked, PICKED0 + NCH * t)
                    nc.vector.reduce_max(crowded[:, bass.ds(t, 1)], cand[:, b, :, CAND - 1], AX_X).then_inc(listed, 1)
                elif n == OPS - 1:
                    dve.wait_ge(listed, at)
                    nc.vector.tensor_copy(keys[:, bass.ds(t, 1), :].rearrange("p o k -> p (o k)"), top[:]).then_inc(listed, 1)
                else:
                    settled(at)
                    left = flat if m < 2 else rest[:, (m // 2 - 1) % 2, :]
                    best = top[:, m // 2 * CAND:(m // 2 + 1) * CAND]
                    if m % 2 == 0:
                        nc.vector.max(best, left).then_inc(listed, 1)
                    else:
                        nc.vector.match_replace(rest[:, m // 2 % 2, :], best, left, imm_value=-2.0 * N).then_inc(listed, 1)

            dve.sem_inc(picked, PICKED0)
            dve.sem_inc(listed, LISTED0)
            nc.vector.memset(cand[:, 1], 0.0).then_inc(blank, 1)
            dve.wait_ge(blank, 1)
            with dve.Fori(0, NT // 2) as i:
                for b in range(2):
                    t = 2 * i + b
                    for c in range(NCH):
                        dve.wait_ge(keyed, KEYED0 + NCH * t + c + 1)
                        dve.nop(nofuse=True)
                        for w in range(NB):
                            op = nc.vector.max(cand[:, b, c * NB + w, :], ps[c % 2][:, w, :])
                            if w == NB - 1:
                                op.then_inc(picked, 1)
                            if c * NB + w < OPS:
                                listing(c * NB + w, t, 1 - b)
                    for n in range(NCH * NB, OPS):
                        listing(n, t, 1 - b)
            for n in range(OPS):
                listing(n, NT, 1)


def order_rows(nc, const, keys, crowded, records, gathers_of, overflow):
    NT = keys.shape[1] - 1
    N = NT * P
    keys, crowded = keys[:, 1:NT + 1, :], crowded[:, 1:NT + 1]
    FAR = float(1 << 20)
    BANK = 512
    with ExitStack() as ctx:
        def sb(name, shape, dt=F32):
            return ctx.enter_context(nc.sbuf_tensor(name, shape, dt))

        def sem(name):
            return signal(nc, const, name)

        valid = sb("o_valid", [P, NT, SLOTS])
        far = sb("o_far", [P, NT, SLOTS])
        degree = sb("o_degree", [P, NT])
        bounded = sb("o_bounded", [P, NT])
        rec = sb("o_rec", [P, NT, REC], I32)
        falling = sb("o_falling", [P, SLOTS])
        member = sb("o_member", [P, SLOTS, NT], BF16)
        ones_bf = sb("o_ones_bf", [P, P], BF16)
        after = sb("o_after", [P, P], BF16)
        one = sb("o_one", [P, 1])
        upto = sb("o_upto", [P, SLOTS * NT])
        rank = sb("o_rank", [P, NT])
        rank_i = sb("o_rank_i", [P, NT], U32)
        most = sb("o_most", [P, 4])
        head = sb("o_head", [1, NT])
        taken = sb("o_taken", [1, NT])
        ps_u = ctx.enter_context(nc.psum_tensor("o_ps_u", [P, SLOTS * NT], F32))
        ps_t = ctx.enter_context(nc.psum_tensor("o_ps_t", [P, SLOTS * NT], F32))
        drawn = sem("o_drawn")
        blank = sem("o_blank")
        step = sem("o_step")
        member_ready = sem("o_member_ready")
        counted = sem("o_counted")
        ranked = sem("o_ranked")
        scattered = sem("o_scattered")
        head_loaded = sem("o_head_loaded")
        most_ready = sem("o_most_ready")
        most_summed = sem("o_most_summed")
        block = ctx.enter_context(nc.Block())

        @block.gpsimd
        def _(pool):
            nc.gpsimd.memset(rec[:], 0).then_inc(blank, 1)
            nc.gpsimd.memset(ones_bf[:], 1.0).then_inc(blank, 1)
            nc.gpsimd.memset(one[:], 1.0).then_inc(blank, 1)
            pool.wait_ge(blank, 3)
            nc.gpsimd.affine_select(out=after[:], in_=ones_bf[:], compare_op=ALU.is_ge, fill=0.0,
                                    base=0, pattern=[[-1, P]], channel_multiplier=1).then_inc(drawn, 1)
            nc.gpsimd.iota(falling[:], [[-1, SLOTS]], base=SLOTS - 1, channel_multiplier=0,
                           allow_small_or_imprecise_dtypes=True).then_inc(drawn, 1)
            nc.gpsimd.iota(const["slot"][:], [[1, SLOTS]], base=0, channel_multiplier=0,
                           allow_small_or_imprecise_dtypes=True).then_inc(drawn, 1)
            nc.gpsimd.iota(rec[:, :, OWN:OWN + 1], [[P, NT]], base=0, channel_multiplier=1).then_inc(drawn, 1)
            pool.wait_ge(ranked, 1)
            pool.wait_ge(drawn, 4)
            for t in range(NT):
                pool.indirect_dma_start(records, bass.IndirectOffsetOnAxis(ap=rank_i[:, t:t + 1], axis=0),
                                        rec[:, t, :], None, bounds_check=N - 1, oob_is_err=False).then_inc(scattered, 16)
            pool.wait_ge(scattered, 16 * NT)
            pool.dma_start(head[:].rearrange("o (t a) -> o t a", a=1),
                           records.bitcast(F32).rearrange("(t p) r -> p t r", p=P)[0:1, :, DEG:DEG + 1],
                           allow_slow_non_contiguous=True).then_inc(head_loaded, 16)

        @block.tensor
        def _(pe):
            pe.wait_ge(member_ready, 1)
            pe.wait_ge(drawn, 1)
            flat = member[:].rearrange("p c t -> p (c t)")
            for b in range(0, SLOTS * NT, BANK):
                w = min(BANK, SLOTS * NT - b)
                nc.tensor.matmul(ps_u[:, b:b + w], after[:], flat[:, b:b + w], start=True, stop=True)
            for b in range(0, SLOTS * NT, BANK):
                w = min(BANK, SLOTS * NT - b)
                op = nc.tensor.matmul(ps_t[:, b:b + w], ones_bf[:], flat[:, b:b + w], start=True, stop=True)
            op.then_inc(counted, 1)
            pe.wait_ge(most_ready, 1)
            nc.tensor.matmul(ps_t[0:1, 0:1], most[:, 3:4], one[:], start=True, stop=True).then_inc(most_summed, 1)

        @block.vector
        def _(dve):
            chain = [0]

            def link(op):
                chain[0] += 1
                op.then_inc(step, 1)
                dve.wait_ge(step, chain[0])

            link(nc.vector.tensor_scalar(valid[:], keys, float(N), None, ALU.is_ge))
            link(nc.vector.reduce_sum(degree[:], valid[:], AX_X))
            link(nc.vector.tensor_scalar(bounded[:], degree[:], float(SLOTS - 1), None, ALU.min))
            dve.wait_ge(drawn, 4)
            nc.vector.tensor_tensor(member[:], falling[:].unsqueeze(2).to_broadcast([P, SLOTS, NT]),
                                    bounded[:].unsqueeze(1).to_broadcast([P, SLOTS, NT]), ALU.is_equal).then_inc(member_ready, 1)
            link(nc.vector.scalar_tensor_tensor(far[:], valid[:], -FAR, keys, ALU.mult, ALU.add))
            link(nc.vector.tensor_scalar(rec[:, :, 0:SLOTS], far[:], FAR - N, None, ALU.add))
            link(nc.vector.tensor_copy(rec[:].bitcast(F32)[:, :, DEG], degree[:]))
            link(nc.vector.reduce_max(most[:, 0:1], crowded, AX_X))
            link(nc.vector.reduce_max(most[:, 1:2], degree[:], AX_X))
            link(nc.vector.tensor_scalar(most[:, 2:3], most[:, 0:1], float(N), None, ALU.is_ge))
            link(nc.vector.tensor_scalar(most[:, 3:4], most[:, 1:2], float(SLOTS), most[:, 2:3], ALU.is_ge, ALU.max))
            dve.wait_ge(counted, 1)
            link(nc.vector.tensor_tensor_scan(upto[:], one[:].to_broadcast([P, SLOTS * NT]), ps_t[:], 0.0, ALU.mult, ALU.add))
            dve.sem_inc(most_ready, 1)
            link(nc.vector.tensor_tensor(upto[:], upto[:], ps_u[:], ALU.subtract))
            link(nc.vector.tensor_tensor(upto[:], upto[:], member[:].rearrange("p c t -> p (c t)"), ALU.mult))
            link(nc.vector.reduce_sum(rank[:], upto[:].rearrange("p (c t) -> p t c", t=NT), AX_X))
            link(nc.vector.tensor_copy(rank_i[:], rank[:]))
            dve.sem_inc(ranked, 1)
            dve.wait_ge(most_summed, 1)
            link(nc.vector.tensor_copy(overflow[:], ps_t[0:1, 0:1]))
            dve.wait_ge(head_loaded, 16)
            link(nc.vector.tensor_copy(gathers_of[0:1, :, 0], head[:]))
            link(nc.vector.tensor_scalar(head[:], head[:], 1.0, 16.0, ALU.add, ALU.mult))
            for b in range(2):
                link(nc.vector.tensor_tensor_scan(taken[0:1, b:NT:2], one[0:1, :].to_broadcast([1, NT // 2]),
                                                  head[0:1, b:NT:2], 0.0, ALU.mult, ALU.add))
            link(nc.vector.tensor_copy(gathers_of[0:1, :, 1], taken[:]))


def sparse_attention(nc, const, layer, table, self_rows, records, gathers_of, dst):
    N = table.shape[0]
    NT = N // P
    BIG = -2.0 * NEG
    W4 = 4
    rec_v = records.rearrange("(t p) r -> t p r", p=P)
    slot, mean_wh = const["slot"], const["mean_wh"]
    with ExitStack() as ctx:
        def sb(name, shape, dt=F32):
            return ctx.enter_context(nc.sbuf_tensor(f"{name}{layer}", shape, dt))

        def sem(name):
            return signal(nc, const, f"{name}{layer}")

        rec = sb("a_rec", [P, 2, REC], I32)
        near = [sb(f"a_near{b}_", [P, SLOTS, ROW]) for b in range(2)]
        own = [sb(f"a_own{b}_", [P, ROW]) for b in range(2)]
        own_i = sb("a_own_i", [P, 2], U32)
        pen = sb("a_pen", [P, SLOTS])
        alone = sb("a_alone", [P, 1])
        base = sb("a_base", [P, D])
        e = sb("a_e", [P, SLOTS])
        neg_max = sb("a_negmax", [P, 1])
        p_all = sb("a_p_all", [P, SLOTS])
        p = sb("a_p", [P, SLOTS])
        den = sb("a_den", [P, 1])
        rden = sb("a_rden", [P, 1])
        parts = sb("a_parts", [P, SLOTS, D])
        o = sb("a_o", [P, D])
        low = sb("a_low", [P, D])
        ex = sb("a_ex", [P, D])
        res = sb("a_res", [P, D])
        fin = sb("a_fin", [P, 2, D])
        rec_loaded = [sem(f"a_rec_loaded{b}_") for b in range(2)]
        rec_free = sem("a_rec_free")
        near_free = sem("a_near_free")
        gathered = [sem(f"a_gathered{b}_") for b in range(2)]
        scattered = [sem(f"a_scattered{b}_") for b in range(2)]
        out_free = sem("a_out_free")
        cleared = sem("a_cleared")
        step = sem("a_step")
        weighed = sem("a_weighed")
        warm = sb("a_warm", [P, 1])
        warmed = sem("a_warmed")
        summed = sem("a_summed")
        max_ready = sem("a_max_ready")
        exp_ready = sem("a_exp_ready")
        low_ready = sem("a_low_ready")
        ex_ready = sem("a_ex_ready")
        fin_ready = sem("a_fin_ready")
        block = ctx.enter_context(nc.Block())

        @block.sync
        def _(sp):
            with sp.Fori(0, NT // 2) as i:
                for b in range(2):
                    sp.wait_ge(rec_free, 2 * i + b + 1)
                    sp.dma_start(rec[:, b, :], rec_v[bass.ds(2 * i + b, 1)].rearrange("o p r -> (o p) r")).then_inc(rec_loaded[b], 16)

        @block.gpsimd
        def _(pool):
            for b in range(2):
                nc.gpsimd.memset(near[b][:], 0.0).then_inc(cleared, 1)
            pool.wait_ge(cleared, 2)
            pool.sem_inc(near_free, 2)
            pool.sem_inc(out_free, 2)

            def gather(t, turn, b):
                index = rec[:, b, :].bitcast(U32)
                count = pool.value_load(gathers_of[0:1, bass.ds(t, 1), 0], min_val=0, max_val=SLOTS)
                pool.wait_ge(rec_loaded[b], 16 * turn + 16)
                pool.nop(nofuse=True)
                pool.wait_ge(near_free, t + 1)
                pool.nop(nofuse=True)

                def one(out, src, k):
                    pool.indirect_dma_start(out, None, src, bass.IndirectOffsetOnAxis(ap=index[:, k:k + 1], axis=0),
                                            bounds_check=N - 1, oob_is_err=False).then_inc(gathered[b], 16)

                one(own[b][:], self_rows, OWN)

                def slots_from(k):
                    with pool.If(count > k):
                        one(near[b][:, k, :], table, k)
                        if k + 1 < SLOTS:
                            slots_from(k + 1)

                slots_from(0)

            def scatter(t, b):
                pool.wait_ge(fin_ready, t + 1)
                pool.nop(nofuse=True)
                pool.indirect_dma_start(dst, bass.IndirectOffsetOnAxis(ap=own_i[:, b:b + 1], axis=0),
                                        fin[:, b, :], None, bounds_check=N - 1, oob_is_err=False).then_inc(scattered[b], 16)

            gather(0, 0, 0)
            with pool.Fori(0, NT // 2 - 1) as i:
                gather(2 * i + 1, i, 1)
                scatter(2 * i, 0)
                gather(2 * i + 2, i + 1, 0)
                scatter(2 * i + 1, 1)
                for b in range(2):
                    pool.wait_ge(scattered[b], 16 * i + 16)
                    pool.sem_inc(out_free, 1)
            gather(NT - 1, NT // 2 - 1, 1)
            scatter(NT - 2, 0)
            scatter(NT - 1, 1)
            for b in range(2):
                pool.wait_ge(scattered[b], 16 * (NT // 2))

        @block.vector
        def _(dve):
            STEPS = 11
            dve.sem_inc(rec_free, 2)
            dve.wait_ge(cleared, 2)
            with dve.Fori(0, NT // 2) as i:
                for b in range(2):
                    t = 2 * i + b
                    chain = [0]

                    def link(op):
                        chain[0] += 1
                        op.then_inc(step, 1)
                        dve.wait_ge(step, STEPS * t + chain[0])

                    def aside(op):
                        chain[0] += 1
                        op.then_inc(step, 1)

                    count = dve.value_load(gathers_of[0:1, bass.ds(t, 1), 0], min_val=0, max_val=SLOTS)
                    taken = dve.value_load(gathers_of[0:1, bass.ds(t, 1), 1], min_val=16, max_val=16 * (SLOTS + 1) * NT)
                    degree = rec[:, b, :].bitcast(F32)[:, DEG:DEG + 1]
                    dve.wait_ge(rec_loaded[b], 16 * i + 16)
                    dve.wait_ge(out_free, t + 1)
                    aside(nc.vector.tensor_copy(own_i[:, b:b + 1], rec[:, b, :].bitcast(U32)[:, OWN:OWN + 1]))
                    aside(nc.vector.tensor_scalar(pen[:], slot[:], degree, BIG, ALU.is_lt, ALU.mult))
                    link(nc.vector.tensor_scalar(alone[:], degree, 0.0, None, ALU.is_equal))
                    aside(nc.vector.tensor_scalar(base[:], mean_wh[:], alone[:, 0:1], None, ALU.mult))
                    dve.wait_ge(gathered[b], taken)
                    link(nc.vector.tensor_scalar(e[:], near[b][:, :, S2], own[b][:, D:D + 1], None, ALU.add))
                    link(nc.vector.scalar_tensor_tensor(e[:], e[:], ALPHA, e[:], ALU.mult, ALU.max))
                    link(nc.vector.scalar_tensor_tensor(e[:], pen[:], NEG, e[:], ALU.add, ALU.min))
                    nc.vector.tensor_reduce(neg_max[:], e[:], AX_X, ALU.max, negate=True).then_inc(max_ready, 1)
                    dve.wait_ge(exp_ready, t + 1)
                    link(nc.vector.scalar_tensor_tensor(p[:], slot[:], degree, p_all[:], ALU.is_lt, ALU.mult, accum_out=den[:]))
                    link(nc.vector.tensor_scalar(den[:], den[:], alone[:, 0:1], None, ALU.add))
                    link(nc.vector.reciprocal(rden[:], den[:]))
                    link(nc.vector.tensor_scalar(p[:], p[:], rden[:, 0:1], None, ALU.mult))
                    assert chain[0] == STEPS
                    dve.sem_inc(rec_free, 1)

                    def weigh(width):
                        nc.vector.tensor_tensor(parts[:, 0:width, :], near[b][:, 0:width, 0:D],
                                                p[:, 0:width].unsqueeze(2).to_broadcast([P, width, D]), ALU.mult).then_inc(weighed, 1)
                        dve.wait_ge(weighed, 2 * t + 1)
                        nc.vector.reduce_sum(o[:], parts[:, 0:width, :].rearrange("p k d -> p d k"), AX_X).then_inc(weighed, 1)

                    for width in range(W4, SLOTS + 1, W4):
                        if width == W4:
                            with dve.If(count < W4 + 1):
                                weigh(width)
                        else:
                            with dve.If(count > width - W4):
                                with dve.If(count < width + 1):
                                    weigh(width)
                    dve.wait_ge(weighed, 2 * t + 2)
                    nc.vector.tensor_tensor(o[:], o[:], base[:], ALU.add).then_inc(summed, 1)
                    dve.wait_ge(summed, 2 * t + 1)
                    nc.vector.tensor_scalar(low[:], o[:], 0.0, None, ALU.min).then_inc(low_ready, 1)
                    nc.vector.scalar_tensor_tensor(res[:], o[:], 0.0, own[b][:, 0:D], ALU.max, ALU.add).then_inc(summed, 1)
                    dve.wait_ge(summed, 2 * t + 2)
                    dve.sem_inc(near_free, 1)
                    dve.wait_ge(ex_ready, t + 1)
                    nc.vector.scalar_tensor_tensor(fin[:, b, :], ex[:], -1.0, res[:], ALU.add, ALU.add).then_inc(fin_ready, 1)

        @block.scalar
        def _(act):
            nc.scalar.activation(warm[:], const["eps"][:], ACT.Exp).then_inc(warmed, 1)
            with act.Fori(0, NT) as t:
                act.wait_ge(max_ready, t + 1)
                nc.scalar.activation(p_all[:], e[:], ACT.Exp, bias=neg_max[:, 0:1]).then_inc(exp_ready, 1)
                act.wait_ge(low_ready, t + 1)
                nc.scalar.activation(ex[:], low[:], ACT.Exp).then_inc(ex_ready, 1)



def gat_kernel(nc, x, adj, W0, a0, W1, a1, out):
    N = x.shape[0]
    table = [nc.dram_tensor(f"table{l}", [N, ROW], F32, kind="Internal").ap() for l in range(2)]
    s2_line = [nc.dram_tensor(f"s2_line{l}", [1, N], F32, kind="Internal").ap() for l in range(2)]
    self_rows = [nc.dram_tensor(f"self_rows{l}", [N, ROW], F32, kind="Internal").ap() for l in range(2)]
    x_mid = nc.dram_tensor("x_mid", [N, D], F32, kind="Internal").ap()
    with ExitStack() as ctx:
        def sb(name, shape, dt=F32):
            return ctx.enter_context(nc.sbuf_tensor(name, shape, dt))

        const = {
            "ident": sb("ident", [P, P]),
            "waug": sb("waug", [P, 2, AUG]),
            "eps": sb("eps", [P, 1]),
            "mean_wh": sb("mean_wh", [P, D]),
            "slot": sb("slot", [P, SLOTS]),
            "signals": [],
        }
        weights_stage(nc, const, [W0, W1], [a0, a1])
        node_transform(nc, const, 0, x, table[0], self_rows[0], s2_line[0])
        NT = N // P
        records = nc.dram_tensor("records", [N, REC], I32, kind="Internal").ap()
        gathers_of = sb("gathers_of", [1, NT, 2], I32)
        overflow = sb("overflow", [1, 1], I32)
        with ExitStack() as lists:
            keys = lists.enter_context(nc.sbuf_tensor("keys", [P, NT + 1, SLOTS], F32))
            crowded = lists.enter_context(nc.sbuf_tensor("crowded", [P, NT + 1], F32))
            scan_edges(nc, const, adj, keys, crowded)
            order_rows(nc, const, keys, crowded, records, gathers_of, overflow)
        sparse_attention(nc, const, 0, table[0], self_rows[0], records, gathers_of, x_mid)
        node_transform(nc, const, 1, x_mid, table[1], self_rows[1], s2_line[1])
        sparse_attention(nc, const, 1, table[1], self_rows[1], records, gathers_of, out)
        nc.clear_and_free_semaphores(const["signals"])
        nc.all_engine_barrier()
        dense_attention(nc, const, 0, table[0], s2_line[0], adj, x, x_mid, overflow)
        node_transform(nc, const, 1, x_mid, table[1], self_rows[1], s2_line[1], overflow)
        dense_attention(nc, const, 1, table[1], s2_line[1], adj, x_mid, out, overflow)


_INS = ["x", "adj", "L0_gnn_W", "L0_gnn_a", "L1_gnn_W", "L1_gnn_a"]


def kernel(**inputs):
    import numpy as _np
    import concourse.bacc as _bacc
    from concourse import mybir as _mybir
    from concourse.bass_utils import run_bass_kernel_spmd as _run

    nc = _bacc.Bacc("TRN2", target_bir_lowering=False, num_devices=1)
    arrays, args = {}, []
    for name in _INS:
        a = _np.ascontiguousarray(inputs[name])
        arrays[f"in_{name}"] = a
        args.append(nc.dram_tensor(f"in_{name}", a.shape, _mybir.dt.from_np(a.dtype), kind="ExternalInput").ap())
    out = nc.dram_tensor("out", inputs["x"].shape, _mybir.dt.float32, kind="ExternalOutput").ap()
    gat_kernel(nc, *args, out)
    r = _run(nc, [arrays], core_ids=[0])
    return r.results[0]["out"]
```

```python
from contextlib import ExitStack, contextmanager

import concourse.bass as bass
from concourse import mybir


P = 128
ALPHA = 0.2
NEG = -9000000000000000.0
EPS = 1e-5

ALU = mybir.AluOpType
ACT = mybir.ActivationFunctionType
F32 = mybir.dt.float32
BF16 = mybir.dt.bfloat16
I32 = mybir.dt.int32
U32 = mybir.dt.uint32
AX_X = mybir.AxisListType.X

D = 128
S2, S1 = D, D + 1
AUG = D + 2
ONE = D + 2
ROW = D + 4

CAND = 8
SLOTS = 32
DEG, OWN = SLOTS, SLOTS + 1
OWN_X = SLOTS + 4
OWN_S1 = OWN_X + D
REC = OWN_X + ROW
CW = 2048
BW = 512
BANKS = 2
W4 = 4
W2 = 2
GROUPS = 4
LAG = 4
LOW = 256


def weights_stage(nc, const, W_dram, a_dram):
    L = len(W_dram)
    ident, waug = const["ident"], const["waug"]
    with ExitStack() as ctx:
        w_t = ctx.enter_context(nc.sbuf_tensor("w_t", [P, L, D], F32))
        a21 = ctx.enter_context(nc.sbuf_tensor("a21", [P, L, 2], F32))
        ps_t = ctx.enter_context(nc.psum_tensor("ps_wt", [P, L, D], F32))
        ps_a = ctx.enter_context(nc.psum_tensor("ps_wa", [P, L, 2], F32))
        loaded = signal(nc, const, "weights_loaded")
        blank = signal(nc, const, "ident_blank")
        drawn = signal(nc, const, "ident_drawn")
        turned = signal(nc, const, "w_turned")
        kept = signal(nc, const, "wt_kept")
        scored = signal(nc, const, "wa_scored")
        done = signal(nc, const, "waug_done")
        block = ctx.enter_context(nc.Block())

        @block.sync
        def _(sp):
            for l in range(L):
                sp.dma_start(waug[:, l, 0:D], W_dram[l]).then_inc(loaded, 16)
                sp.dma_start(a21[:, l, 0:1], a_dram[l][D:2 * D, :]).then_inc(loaded, 16)
                sp.dma_start(a21[:, l, 1:2], a_dram[l][0:D, :]).then_inc(loaded, 16)

        @block.gpsimd
        def _(pool):
            nc.gpsimd.memset(ident[:], 0.0).then_inc(blank, 1)
            pool.wait_ge(blank, 1)
            nc.gpsimd.affine_select(out=ident[:], in_=ident[:], compare_op=ALU.not_equal, fill=1.0,
                                    base=0, pattern=[[-1, P]], channel_multiplier=1).then_inc(drawn, 1)

        @block.tensor
        def _(pe):
            pe.wait_ge(loaded, 48 * L)
            pe.wait_ge(drawn, 1)
            for l in range(L):
                nc.tensor.transpose(ps_t[:, l, :], waug[:, l, 0:D], ident[:]).then_inc(turned, 1)
            pe.wait_ge(kept, 1)
            for l in range(L):
                nc.tensor.matmul(ps_a[:, l, :], w_t[:, l, :], a21[:, l, :], start=True, stop=True).then_inc(scored, 1)

        @block.vector
        def _(dve):
            nc.vector.memset(const["eps"][:], EPS).then_inc(done, 1)
            dve.wait_ge(turned, L)
            nc.vector.tensor_copy(w_t[:], ps_t[:]).then_inc(kept, 1)
            dve.wait_ge(scored, L)
            nc.vector.tensor_copy(waug[:, :, S2:AUG], ps_a[:]).then_inc(done, 1)


def signal(nc, const, name):
    const["signals"].append(nc.alloc_semaphore(name))
    return const["signals"][-1]


@contextmanager
def when(engine, flag):
    if flag is None:
        yield
    else:
        with engine.If(engine.value_load(flag[0:1, 0:1], min_val=0, max_val=P) > 0):
            yield


def node_transform(nc, const, layer, x_dram, table, self_rows, s2_line, only_if=None):
    N = x_dram.shape[0]
    tag = "" if only_if is None else "again"
    Q = 4
    STEPS = N // (Q * P)
    x_v = x_dram.rearrange("(s q p) d -> s p q d", q=Q, p=P)
    t_v = table.rearrange("(s q p) d -> s p q d", q=Q, p=P)
    self_v = self_rows.rearrange("(s q p) d -> s p q d", q=Q, p=P)
    mean_wh = const["mean_wh"]
    ident, waug, eps = const["ident"], const["waug"], const["eps"]
    with ExitStack() as ctx:
        def sb(name, shape):
            return ctx.enter_context(nc.sbuf_tensor(f"{name}{tag}{layer}", shape, F32))

        def sem(name):
            return signal(nc, const, f"{name}{tag}{layer}")

        x_in = sb("x_in", [P, 2, Q, ROW])
        x_hat = sb("x_hat", [P, 2, Q, D])
        h_sums = sb("h_sums", [P, STEPS])
        h_sum = sb("h_sum", [P, 1])
        h_sum_wide = sb("h_sum_wide", [P, P])
        stats = sb("stats", [P, 2, Q, 6])
        mv = sb("mv", [P, 2, Q, 2])
        std = sb("std", [P, 2, Q])
        rstd = sb("rstd", [P, 2, Q])
        h_t = sb("h_t", [P, 2, Q, P])
        rows = sb("rows", [P, 2, Q, ROW])
        ps_h = [ctx.enter_context(nc.psum_tensor(f"ps_h{b}_{tag}{layer}", [P, Q, P], F32)) for b in range(2)]
        ps_w = [ctx.enter_context(nc.psum_tensor(f"ps_w{b}_{tag}{layer}", [P, Q, 256], F32)) for b in range(2)]
        summed = sem("h_summed")
        widened = sem("h_widened")
        averaged = sem("averaged")
        mean_ready = sem("mean_ready")
        line = sb("line", [1, 2, Q * P])
        ps_l = [ctx.enter_context(nc.psum_tensor(f"ps_l{b}_{tag}{layer}", [P, Q * P], F32)) for b in range(2)]
        x_loaded = [sem(f"x_loaded{b}_") for b in range(2)]
        x_padded = sem("x_padded")
        warm = sb("warm", [P, 1])
        warmed = sem("warmed")
        x_hat_free = sem("x_hat_free")
        stat = sem("stat")
        aggr = sem("aggr")
        rooted = sem("rooted")
        inverted = sem("inverted")
        normed = sem("normed")
        turned = sem("turned")
        relued = sem("relued")
        multiplied = sem("multiplied")
        row_ready = sem("row_ready")
        padded = sem("padded")
        stored = [sem(f"stored{b}_") for b in range(2)]
        block = ctx.enter_context(nc.Block())

        @block.sync
        def _(sp):
            with when(sp, only_if):
                with sp.Fori(0, STEPS // 2) as i:
                    for b in range(2):
                        sp.wait_ge(x_padded, 1)
                        sp.wait_ge(stored[b], 48 * i + 48)
                        sp.dma_start(x_in[:, b, :, 0:D], x_v[bass.ds(2 * i + b, 1)].rearrange("o p q d -> (o p) q d")).then_inc(x_loaded[b], 16)

        @block.vector
        def _(dve):
            with when(dve, only_if):
                nc.vector.memset(rows[:], 1.0).then_inc(padded, 1)
                nc.vector.memset(x_in[:, :, :, D:ROW], 0.0).then_inc(padded, 1)
                dve.wait_ge(padded, 2)
                dve.sem_inc(x_padded, 1)
                with dve.Fori(0, STEPS // 2) as i:
                    for b in range(2):
                        s = 2 * i + b
                        dve.wait_ge(x_loaded[b], 16 * i + 16)
                        for q in range(Q):
                            nc.vector.bn_stats(stats[:, b, q, :], x_in[:, b, q, 0:D]).then_inc(stat, 1)
                        dve.wait_ge(stat, Q * s + Q)
                        dve.nop(nofuse=True)
                        for q in range(Q):
                            nc.vector.bn_aggr(mv[:, b, q, :], stats[:, b, q, :]).then_inc(aggr, 1)
                        dve.wait_ge(rooted, s + 1)
                        nc.vector.reciprocal(rstd[:, b, :], std[:, b, :]).then_inc(inverted, 1)
                        dve.wait_ge(inverted, s + 1)
                        dve.wait_ge(x_hat_free, s + 1)
                        for q in range(Q):
                            op = nc.vector.tensor_scalar(x_hat[:, b, q, :], x_in[:, b, q, 0:D], mv[:, b, q, 0:1],
                                                         rstd[:, b, q:q + 1], ALU.subtract, ALU.mult)
                        op.then_inc(normed, 1)
                dve.wait_ge(relued, STEPS)
                nc.vector.reduce_sum(h_sum[:], h_sums[:], AX_X).then_inc(summed, 1)
                dve.wait_ge(summed, 1)
                nc.vector.tensor_copy(h_sum_wide[:], h_sum[:].to_broadcast([P, P])).then_inc(widened, 1)
                dve.wait_ge(averaged, 1)
                nc.vector.tensor_scalar(mean_wh[:], ps_l[0][:, 0:D], 1.0 / N, None, ALU.mult).then_inc(mean_ready, 1)

        @block.scalar
        def _(act):
            with when(act, only_if):
                act.wait_ge(padded, 2)
                act.sem_inc(x_hat_free, 2)
                nc.scalar.activation(warm[:], eps[:], ACT.Sqrt).then_inc(warmed, 1)
                for b in range(2):
                    act.sem_inc(stored[b], 48)
                with act.Fori(0, STEPS // 2) as i:
                    for b in range(2):
                        s = 2 * i + b
                        act.wait_ge(aggr, Q * s + Q)
                        nc.scalar.activation(std[:, b, :], mv[:, b, :, 1], ACT.Sqrt, bias=eps[:, 0:1]).then_inc(rooted, 1)
                        act.wait_ge(turned, s + 1)
                        nc.scalar.activation(h_t[:, b], ps_h[b][:], ACT.Relu,
                                             accum_out=h_sums[:, bass.ds(s, 1)]).then_inc(relued, 1)
                        act.sem_inc(x_hat_free, 1)
                        act.wait_ge(multiplied, s + 1)
                        act.wait_ge(stored[b], 48 * i + 48)
                        nc.scalar.activation(rows[:, b, :, 0:AUG], ps_w[b][:, :, 0:AUG], ACT.Copy).then_inc(row_ready, 1)
                        nc.scalar.activation(x_in[:, b, :, D:D + 1], ps_w[b][:, :, S1:S1 + 1], ACT.Copy).then_inc(row_ready, 1)
                        nc.scalar.activation(line[:, b], ps_l[b][0:1, :], ACT.Copy).then_inc(row_ready, 1)
                        act.wait_ge(row_ready, 3 * s + 3)
                        act.dma_start(t_v[bass.ds(s, 1)].rearrange("o p q d -> (o p) q d"), rows[:, b]).then_inc(stored[b], 16)
                        act.dma_start(self_v[bass.ds(s, 1)].rearrange("o p q d -> (o p) q d"), x_in[:, b]).then_inc(stored[b], 16)
                        act.dma_start(s2_line[:, bass.ds(s * (Q * P), Q * P)], line[:, b]).then_inc(stored[b], 16)
                for b in range(2):
                    act.wait_ge(stored[b], 48 * (STEPS // 2 + 1))

        @block.tensor
        def _(pe):
            with when(pe, only_if):
                with pe.Fori(0, STEPS // 2) as i:
                    for b in range(2):
                        s = 2 * i + b
                        pe.wait_ge(normed, s + 1)
                        for q in range(Q):
                            op = nc.tensor.transpose(ps_h[b][:, q, :], x_hat[:, b, q, :], ident[:])
                        op.then_inc(turned, 1)
                        pe.wait_ge(relued, s + 1)
                        for q in range(Q):
                            op = nc.tensor.matmul(ps_w[b][:, q, 0:AUG], h_t[:, b, q, :], waug[:, layer, :], start=True, stop=True)
                        op = nc.tensor.matmul(ps_l[b][0:1, :], waug[:, layer, S2:S2 + 1], h_t[:, b].rearrange("p q n -> p (q n)"),
                                              start=True, stop=True)
                        op.then_inc(multiplied, 1)
                pe.wait_ge(widened, 1)
                pe.wait_ge(row_ready, 3 * STEPS)
                nc.tensor.matmul(ps_l[0][:, 0:D], h_sum_wide[:], waug[:, layer, 0:D], start=True, stop=True).then_inc(averaged, 1)


def dense_attention(nc, const, layer, table, s2_line, adj, x_dram, dst, only_if=None):
    N = x_dram.shape[0]
    NB = N // P
    CW = 2048
    NCH = N // CW
    EW = 512
    NE = N // EW
    KQ = EW // P
    BIG = -2.0 * NEG
    ident = const["ident"]
    x_v = x_dram.rearrange("(t p) d -> t p d", p=P)
    dst_v = dst.rearrange("(t p) d -> t p d", p=P)
    adj_v = adj.rearrange("(t p) (c w) -> t c p w", p=P, w=CW)
    t_v = table.rearrange("(t p) d -> p t d", p=P)
    with ExitStack() as ctx:
        def sb(name, shape, dt=F32):
            return ctx.enter_context(nc.sbuf_tensor(f"{name}{layer}", shape, dt))

        def sem(name):
            return signal(nc, const, f"{name}{layer}")

        wh = sb("d_wh", [P, NB, ROW])
        s2b = sb("d_s2b", [P, N])
        adj_in = sb("d_adj", [P, NCH, CW], I32)
        pen = sb("d_pen", [P, CW])
        e = sb("d_e", [P, N])
        mx = sb("d_mx", [P, NCH])
        neg_max = sb("d_negmax", [P, 1])
        p_row = sb("d_p", [P, 2, EW])
        p_t = sb("d_pt", [P, 2, KQ, P])
        x_in = sb("d_x", [P, D])
        rden = sb("d_rden", [P, 1])
        o = sb("d_o", [P, D])
        low = sb("d_low", [P, D])
        ex = sb("d_ex", [P, D])
        res = sb("d_res", [P, D])
        fin = sb("d_fin", [P, D])
        ps_t = [ctx.enter_context(nc.psum_tensor(f"d_pst{b}_{layer}", [P, KQ, P], F32)) for b in range(2)]
        ps_o = ctx.enter_context(nc.psum_tensor(f"d_pso_{layer}", [P, ONE + 1], F32))
        resident = sem("d_resident")
        adj_loaded = [sem(f"d_adj_loaded{c}_") for c in range(NCH)]
        adj_free = sem("d_adj_free")
        x_loaded = sem("d_x_loaded")
        x_free = sem("d_x_free")
        step = sem("d_step")
        maxed = sem("d_maxed")
        exped = sem("d_exped")
        e_free = sem("d_e_free")
        turned = sem("d_turned")
        kept = sem("d_kept")
        summed = sem("d_summed")
        o_step = sem("d_o_step")
        low_ready = sem("d_low_ready")
        ex_ready = sem("d_ex_ready")
        fin_ready = sem("d_fin_ready")
        stored = sem("d_stored")
        block = ctx.enter_context(nc.Block())
        C_STEP = 4 * NCH

        @block.sync
        def _(sp):
            with when(sp, only_if):
                sp.dma_start(wh[:], t_v).then_inc(resident, 16)
                sp.dma_start(s2b[:], s2_line.to_broadcast([P, N])).then_inc(resident, 16)
                with sp.Fori(0, NB) as t:
                    for c in range(NCH):
                        sp.wait_ge(adj_free, NCH * t + c + 1)
                        sp.dma_start(adj_in[:, c, :], adj_v[bass.ds(t, 1), c].rearrange("o p w -> (o p) w")).then_inc(adj_loaded[c], 16)
                    sp.wait_ge(x_free, t + 1)
                    sp.dma_start(x_in[:], x_v[bass.ds(t, 1)].rearrange("o p d -> (o p) d")).then_inc(x_loaded, 16)
                    sp.wait_ge(fin_ready, t + 1)
                    sp.dma_start(dst_v[bass.ds(t, 1)].rearrange("o p d -> (o p) d"), fin[:]).then_inc(stored, 16)
                sp.wait_ge(stored, 16 * NB + 16)

        @block.vector
        def _(dve):
            with when(dve, only_if):
                dve.sem_inc(adj_free, NCH)
                dve.sem_inc(x_free, 1)
                dve.sem_inc(stored, 16)
                dve.wait_ge(resident, 32)
                with dve.Fori(0, NB) as t:
                    dve.wait_ge(e_free, t + 1)
                    for c in range(NCH):
                        ec = e[:, c * CW:(c + 1) * CW]
                        nc.vector.tensor_scalar(ec, s2b[:, c * CW:(c + 1) * CW], wh[:, bass.ds(t, 1), S1], None, ALU.add).then_inc(step, 1)
                        dve.wait_ge(step, C_STEP * t + 4 * c + 1)
                        nc.vector.scalar_tensor_tensor(ec, ec, ALPHA, ec, ALU.mult, ALU.max).then_inc(step, 1)
                        dve.wait_ge(adj_loaded[c], 16 * t + 16)
                        nc.vector.tensor_scalar(pen[:], adj_in[:, c, :], 0, BIG, ALU.is_gt, ALU.mult).then_inc(step, 1)
                        dve.wait_ge(step, C_STEP * t + 4 * c + 3)
                        dve.sem_inc(adj_free, 1)
                        nc.vector.scalar_tensor_tensor(ec, pen[:], NEG, ec, ALU.add, ALU.min).then_inc(step, 1)
                        dve.wait_ge(step, C_STEP * t + 4 * c + 4)
                        op = nc.vector.reduce_max(mx[:, c:c + 1], ec, AX_X)
                        op.then_inc(maxed, 1)
                    dve.wait_ge(maxed, (NCH + 1) * t + NCH)
                    nc.vector.tensor_reduce(neg_max[:], mx[:], AX_X, ALU.max, negate=True).then_inc(maxed, 1)
                    for c in range(NE):
                        dve.wait_ge(turned, NE * t + c + 1)
                        nc.vector.tensor_copy(p_t[:, c % 2], ps_t[c % 2][:]).then_inc(kept, 1)
                    dve.wait_ge(summed, t + 1)
                    nc.vector.reciprocal(rden[:], ps_o[:, ONE:ONE + 1]).then_inc(o_step, 1)
                    dve.wait_ge(o_step, 2 * t + 1)
                    nc.vector.tensor_scalar(o[:], ps_o[:, 0:D], rden[:, 0:1], None, ALU.mult).then_inc(o_step, 1)
                    dve.wait_ge(o_step, 2 * t + 2)
                    nc.vector.tensor_scalar(low[:], o[:], 0.0, None, ALU.min).then_inc(low_ready, 1)
                    dve.wait_ge(x_loaded, 16 * t + 16)
                    nc.vector.scalar_tensor_tensor(res[:], o[:], 0.0, x_in[:], ALU.max, ALU.add).then_inc(x_free, 1)
                    dve.wait_ge(x_free, t + 2)
                    dve.wait_ge(ex_ready, t + 1)
                    dve.wait_ge(stored, 16 * t + 16)
                    nc.vector.scalar_tensor_tensor(fin[:], ex[:], -1.0, res[:], ALU.add, ALU.add).then_inc(fin_ready, 1)

        @block.scalar
        def _(act):
            with when(act, only_if):
                act.sem_inc(e_free, 1)
                with act.Fori(0, NB) as t:
                    act.wait_ge(maxed, (NCH + 1) * t + NCH + 1)
                    for c in range(NE):
                        act.wait_ge(turned, NE * t + c + 1 - 2) if c >= 2 else None
                        nc.scalar.activation(p_row[:, c % 2, :], e[:, c * EW:(c + 1) * EW], ACT.Exp,
                                             bias=neg_max[:, 0:1]).then_inc(exped, 1)
                    act.wait_ge(exped, NE * t + NE)
                    act.sem_inc(e_free, 1)
                    act.wait_ge(low_ready, t + 1)
                    nc.scalar.activation(ex[:], low[:], ACT.Exp).then_inc(ex_ready, 1)

        @block.tensor
        def _(pe):
            with when(pe, only_if):
                pe.wait_ge(resident, 32)

                def product(t, c):
                    pe.wait_ge(kept, NE * t + c + 1)
                    for q in range(KQ):
                        op = nc.tensor.matmul(ps_o[:], p_t[:, c % 2, q, :], wh[:, KQ * c + q, 0:ONE + 1],
                                              start=(c == 0 and q == 0), stop=(c == NE - 1 and q == KQ - 1))
                    if c == NE - 1:
                        op.then_inc(summed, 1)

                with pe.Fori(0, NB) as t:
                    for c in range(NE):
                        pe.wait_ge(exped, NE * t + c + 1)
                        for q in range(KQ):
                            op = nc.tensor.transpose(ps_t[c % 2][:, q, :], p_row[:, c % 2, q * P:(q + 1) * P], ident[:])
                        op.then_inc(turned, 1)
                        if c >= 1:
                            product(t, c - 1)
                    product(t, NE - 1)

def signals(nc, stage, names):
    return {n: nc.alloc_semaphore(f"{n}_{stage}") for n in names}


def finish(nc, sems):
    nc.clear_and_free_semaphores(list(sems.values()))
    nc.all_engine_barrier()


def constants_stage(nc, const, N):
    NT = N // P
    GT = NT // GROUPS
    s = signals(nc, "const", ["c_blank", "c_numbered", "c_spread", "c_drawn", "c_moved"])
    blank, numbered, spread, drawn, moved = (s[n] for n in ("c_blank", "c_numbered", "c_spread", "c_drawn", "c_moved"))
    col, lift, ones_bf, after = const["col"], const["lift"], const["ones_bf"], const["after"]
    with ExitStack() as ctx:
        low = ctx.enter_context(nc.sbuf_tensor("low_part", [1, LOW], BF16))
        high = ctx.enter_context(nc.sbuf_tensor("high_part", [1, N // LOW], BF16))
        col_high = ctx.enter_context(nc.sbuf_tensor("col_high", [1, N], BF16))
        block = ctx.enter_context(nc.Block())

        @block.vector
        def _(dve):
            nc.vector.memset(lift[:], 0.0).then_inc(blank, 1)
            nc.vector.memset(ones_bf[:], 1.0).then_inc(blank, 1)
            nc.vector.memset(col[:], 0.0).then_inc(blank, 1)
            dve.wait_ge(blank, 3)
            dve.wait_ge(numbered, 2)
            nc.vector.tensor_copy(col[0:1, :].rearrange("o (h l) -> o h l", l=LOW),
                                  low[:].unsqueeze(1).to_broadcast([1, N // LOW, LOW])).then_inc(spread, 1)
            for b in range(2):
                nc.vector.memset(const["cand"][:, b], 0.0).then_inc(spread, 1)
            nc.vector.memset(const["one"][:], 1.0).then_inc(spread, 1)

        @block.scalar
        def _(act):
            act.wait_ge(numbered, 2)
            nc.scalar.activation(col_high[:].rearrange("o (h l) -> o h l", l=LOW),
                                 high[:].unsqueeze(2).to_broadcast([1, N // LOW, LOW]), ACT.Copy).then_inc(moved, 1)

        @block.gpsimd
        def _(pool):
            nc.gpsimd.iota(low[:], [[1, LOW]], base=0, channel_multiplier=0,
                           allow_small_or_imprecise_dtypes=True).then_inc(numbered, 1)
            nc.gpsimd.iota(high[:], [[LOW, N // LOW]], base=0, channel_multiplier=0,
                           allow_small_or_imprecise_dtypes=True).then_inc(numbered, 1)
            pool.wait_ge(blank, 2)
            nc.gpsimd.affine_select(out=lift[:], in_=lift[:], compare_op=ALU.not_equal, fill=float(N),
                                    base=0, pattern=[[-1, P]], channel_multiplier=1).then_inc(drawn, 1)
            nc.gpsimd.affine_select(out=after[:], in_=ones_bf[:], compare_op=ALU.is_ge, fill=0.0,
                                    base=0, pattern=[[-1, P]], channel_multiplier=1).then_inc(drawn, 1)
            nc.gpsimd.iota(const["falling"][:], [[-1, SLOTS]], base=SLOTS - 1, channel_multiplier=0,
                           allow_small_or_imprecise_dtypes=True).then_inc(drawn, 1)
            nc.gpsimd.iota(const["slot"][:], [[1, SLOTS]], base=0, channel_multiplier=0,
                           allow_small_or_imprecise_dtypes=True).then_inc(drawn, 1)
            nc.gpsimd.iota(const["first_row"][:], [[P, GT]], base=0, channel_multiplier=0,
                           allow_small_or_imprecise_dtypes=True).then_inc(drawn, 1)
            for b in range(2):
                nc.gpsimd.memset(const["near"][b][:], 0.0).then_inc(drawn, 1)
            nc.gpsimd.memset(const["rec"][:], 0).then_inc(drawn, 1)
            nc.gpsimd.memset(const["lin_rows"][:], 1.0).then_inc(drawn, 1)

        @block.sync
        def _(sp):
            sp.wait_ge(blank, 3)
            sp.wait_ge(moved, 1)
            sp.dma_start(col[1:2, :], col_high[:]).then_inc(moved, 16)
            sp.wait_ge(moved, 17)
    finish(nc, s)


def pipeline_stage(nc, const, stage, x, adj, table, self_rows, records, out, scan=None, transform=False,
                   order=None, attend=None, lin=None, close=False):
    N = adj.shape[0]
    NT = N // P
    GT = NT // GROUPS
    NCH = N // CW
    BPC = CW // BW
    HPC = BPC // BANKS
    HALVES = N // BW // BANKS
    NBLK = N // BW
    ROUNDS = SLOTS // CAND
    OPS = 2 * ROUNDS + 1
    BIG = -2.0 * NEG
    FAR = float(1 << 20)
    Q = 4
    TURNS = 4
    STEPS = max(c for c in (GT if scan is not None or transform else 0,
                            attend[2] if attend else 0, lin[2] if lin else 0))
    layer = attend[0] if attend else 0
    A0, ASKIP = attend[1] if attend else (0, 0)
    AN = attend[2] if attend else 0
    M0, MSKIP = lin[0:2] if lin else (0, 0)
    MN = lin[2] if lin else 0
    ident, waug, eps, slot = const["ident"], const["waug"], const["eps"], const["slot"]
    mean_wh = const["mean_wh"]
    keys, crowded, cand = const["keys"], const["crowded"], const["cand"]
    rec, rec_all, near = const["rec"], const["rec_all"], const["near"]
    rec_f, all_f = rec[:].bitcast(F32), rec_all[:].bitcast(F32)
    count_of, head, taken_of = const["count_of"], const["head"], const["taken_of"]
    ps_keys, ps_o, ps_lin, ps_h = const["ps_keys"], const["ps_o"], const["ps_lin"], const["ps_h"]
    adj_in, edge, lin_rows = const["adj_in"], const["edge"], const["lin_rows"]
    mv_all, rstd_all, h_sums = const["mv_all"], const["rstd_all"], const["h_sums"]
    adj_v = adj.rearrange("(t p) (c w) -> t c p w", p=P, w=CW)
    by_tile = lambda ap: ap.rearrange("(t p) d -> p t d", p=P)

    names = ([f"adj_loaded{c}" for c in range(NCH)] + ["edge_ready", "keyed", "picked", "listed"] if scan is not None else [])
    if transform:
        names += ["x_loaded0", "x_loaded1", "padded", "stat", "aggr", "rooted", "inverted", "normed", "turned",
                  "relued", "multiplied", "row_ready", "row_free", "stored0", "stored1"]
    if order is not None:
        names += ["own_loaded", "ids_drawn", "o_step", "member_ready", "counted", "ranked", "rec_scattered",
                  "rec_loaded", "counts_ready"]
    if attend:
        names += ["gathered0", "gathered1", "near_ready", "idx_ready", "step", "max_ready", "exp_ready", "p_ready",
                  "parts_ready", "summed", "o_ready", "low_ready", "ex_ready", "fin_ready", "fin_step", "taken_ready", "taken_step"]
    if lin or (attend and layer == 1):
        names += ["out_scattered0", "out_scattered1"]
    if lin:
        names += ["l_rooted", "l_inverted", "l_normed", "l_named", "l_turned", "l_relued", "l_multiplied", "l_ready"]
    if transform or close:
        names += ["h_summed", "h_widened", "averaged", "mean_ready"]
    if close:
        names += ["flagged", "flags_summed", "overflow_ready"]
    s = signals(nc, stage, names)
    S = lambda n: s[n]

    with ExitStack() as ctx:
        def sb(name, shape, dt=F32):
            return ctx.enter_context(nc.sbuf_tensor(f"{name}_{stage}", shape, dt))

        if scan is not None:
            rest = sb("rest", [P, 2, NBLK * CAND])
            top = sb("top", [P, SLOTS])
        if transform:
            x_in = sb("x_in", [P, 2, Q, ROW])
            x_hat = sb("x_hat", [P, Q, D])
            stats = sb("stats", [P, Q, 6])
            mv = sb("mv", [P, Q, 2])
            std = sb("std", [P, Q])
            rstd = sb("rstd", [P, Q])
            h_t = sb("h_t", [P, Q, P])
            rows = sb("rows", [P, 2, Q, ROW])
            x_v = x.rearrange("(s q p) d -> s p q d", q=Q, p=P)
            t_v = table[0].rearrange("(s q p) d -> s p q d", q=Q, p=P)
            self_v = self_rows.rearrange("(s q p) d -> s p q d", q=Q, p=P)
        if order is not None:
            valid = sb("valid", [P, GT, SLOTS])
            far = sb("far", [P, GT, SLOTS])
            degree = sb("degree", [P, GT])
            bounded = sb("bounded", [P, GT])
            member = sb("member", [P, SLOTS, GT], BF16)
            upto = sb("upto", [P, SLOTS * GT])
            upto_own = sb("upto_own", [P, SLOTS * GT])
            rank = sb("rank", [P, GT])
            rank_i = sb("rank_i", [P, GT], U32)
            most = sb("most", [P, 3])
            above = sb("above", [1, GT, SLOTS - 1])
        if attend:
            idx = [sb(f"idx{b}", [P, SLOTS], U32) for b in range(2)]
            taken = sb("taken", [1, NT])
            taken_sum = sb("taken_sum", [1, NT])
            pen = sb("pen", [P, SLOTS])
            alone = sb("alone", [P, 2])
            base = sb("base", [P, D])
            e = sb("e", [P, SLOTS])
            neg_max = sb("neg_max", [P, 1])
            p_all = sb("p_all", [P, SLOTS])
            p = sb("p", [P, SLOTS])
            den = sb("den", [P, 1])
            rden = sb("rden", [P, 2])
            parts = sb("parts", [P, SLOTS, D])
            o = sb("o", [P, D])
            low = sb("low", [P, D])
            ex = sb("ex", [P, D])
            res = sb("res", [P, D])
            fin = sb("fin", [P, 2, D])
            st = sb("st", [P, 6])
            mv1 = sb("mv1", [P, 2])
        if lin or attend:
            out_idx = sb("out_idx", [P, 2], U32)
        if lin:
            std_all = sb("std_all", [P, MN])
            x_hat1 = sb("x_hat1", [P, 2, D])
            h_t1 = sb("h_t1", [P, 2, D])
        if transform or close:
            h_sum = sb("h_sum", [P, 1])
            h_sum_wide = sb("h_sum_wide", [P, P])
        if close:
            flag = sb("flag", [P, 1])

        block = ctx.enter_context(nc.Block())

        FIRST = max(4 if layer == 1 else 2, LAG if order is not None else 0, ASKIP + 2 if attend else 0, MSKIP + 2 if lin else 0)
        LAST = min([STEPS] + [AN] * (attend is not None) + [MN] * (lin is not None)) - 2

        def steps(engine, body):
            def pair(i, first):
                for b in range(2):
                    body(2 * i + b, i, b, first + b)

            lo, hi = FIRST // 2, LAST // 2
            for i in range(min(lo, hi)):
                pair(i, 2 * i)
            if lo < hi:
                with engine.Fori(lo, hi) as i:
                    pair(i, 2 * lo)
            for i in range(hi, STEPS // 2):
                pair(i, 2 * i)

        def stored(engine, i, b, skip):
            turns = i - skip // 2
            if not isinstance(turns, int) or turns > 0:
                engine.wait_ge(S(f"out_scattered{b}"), 16 * turns)

        def attends(at):
            return attend is not None and ASKIP <= at < AN

        def lins(at):
            return lin is not None and MSKIP <= at < MN

        @block.sync
        def _(sp):
            def own_rows():
                sp.dma_start(rec_f[:, :, OWN_X:REC], by_tile(self_rows)[:, order * GT:(order + 1) * GT, :]).then_inc(S("own_loaded"), 16)

            def near_is_there(step, b, at):
                if at == ASKIP:
                    sp.wait_ge(S("taken_ready"), 1)
                got = sp.value_load(taken_of[0:1, bass.ds(step + A0, 1)], min_val=16, max_val=16 * SLOTS * NT)
                sp.wait_ge(S(f"gathered{b}"), got)
                sp.sem_inc(S("near_ready"), 1)

            def adj_chunks(step, chunks):
                for c in chunks:
                    sp.wait_ge(S("edge_ready"), NCH * step + c + 1)
                    sp.dma_start(adj_in[:, c, :], adj_v[bass.ds(step + scan * GT, 1), c].rearrange("o p w -> (o p) w")).then_inc(S(f"adj_loaded{c}"), 16)

            def body(step, i, b, at):
                if scan is None:
                    if attends(at):
                        near_is_there(step, b, at)
                    return
                if order is not None and at == 1:
                    own_rows()
                adj_chunks(step, range(NCH - 1))
                if attends(at - 1):
                    near_is_there(step - 1, 1 - b, at - 1)
                adj_chunks(step, range(NCH - 1, NCH))

            if order is not None and scan is None:
                own_rows()
            steps(sp, body)
            if scan is not None and attend:
                near_is_there(STEPS - 1, 1, STEPS - 1)

        @block.gpsimd
        def _(pool):
            if transform:
                pool.wait_ge(S("padded"), 2)
                pool.sem_inc(S("row_free"), 2)

                def load_x(step, b):
                    pool.dma_start(x_in[:, b, :, 0:D], x_v[bass.ds(step, 1)].rearrange("o p q d -> (o p) q d")).then_inc(S(f"x_loaded{b}"), 16)

                for b in range(2):
                    load_x(b, b)

                def body(step, i, b, at):
                    pool.wait_ge(S("row_ready"), 2 * step + 2)
                    pool.dma_start(t_v[bass.ds(step, 1)].rearrange("o p q d -> (o p) q d"), rows[:, b]).then_inc(S(f"stored{b}"), 16)
                    pool.dma_start(self_v[bass.ds(step, 1)].rearrange("o p q d -> (o p) q d"), x_in[:, b]).then_inc(S(f"stored{b}"), 16)
                    pool.wait_ge(S(f"stored{b}"), 32 * i + 32)
                    pool.sem_inc(S("row_free"), 1)
                    if at + 2 < GT:
                        load_x(step + 2, b)

                steps(pool, body)

            def order_records():
                pool.wait_ge(S("ranked"), 1)
                pool.wait_ge(S("own_loaded"), 16)
                pool.wait_ge(S("ids_drawn"), 1)
                for t in range(GT):
                    pool.indirect_dma_start(records, bass.IndirectOffsetOnAxis(ap=rank_i[:, t:t + 1], axis=0),
                                            rec[:, t, :], None, bounds_check=N - 1, oob_is_err=False).then_inc(S("rec_scattered"), 16)

            def load_records():
                pool.wait_ge(S("counts_ready"), 1)
                pool.wait_ge(S("rec_scattered"), 16 * GT)
                pool.dma_start(rec_all[:, order * GT:(order + 1) * GT, :],
                               by_tile(records)[:, order * GT:(order + 1) * GT, :]).then_inc(S("rec_loaded"), 16)

            def gather(step, i, b):
                here = step - ASKIP
                count = pool.value_load(count_of[0:1, bass.ds(step + A0, 1)], min_val=0, max_val=SLOTS)
                pool.wait_ge(S("idx_ready"), here + 1)
                pool.nop(nofuse=True)
                pool.wait_ge(S("parts_ready"), here + 1)
                pool.nop(nofuse=True)

                def one(k):
                    pool.indirect_dma_start(near[b][:, k, :], None, table[layer], bass.IndirectOffsetOnAxis(ap=idx[b][:, k:k + 1], axis=0),
                                            bounds_check=N - 1, oob_is_err=False).then_inc(S(f"gathered{b}"), 16)

                def slots_from(k):
                    with pool.If(count > k):
                        one(k)
                        if k + 1 < SLOTS - 1:
                            slots_from(k + 1)

                for k in range(W4):
                    one(k)
                yield
                slots_from(W4)

            def scatter(step, i, b, skip):
                here = step - skip
                if lin:
                    pool.wait_ge(S("l_named"), here + 1)
                    pool.nop(nofuse=True)
                    pool.wait_ge(S("l_ready"), 2 * here + 4)
                    dst, src = table[1], lin_rows[:, b, :]
                else:
                    pool.wait_ge(S("fin_ready"), 2 * here + 2)
                    dst, src = out, fin[:, b, :]
                pool.nop(nofuse=True)
                pool.indirect_dma_start(dst, bass.IndirectOffsetOnAxis(ap=out_idx[:, b:b + 1], axis=0),
                                        src, None, bounds_check=N - 1, oob_is_err=False).then_inc(S(f"out_scattered{b}"), 16)

            puts = lin is not None or (attend is not None and layer == 1)
            skip = MSKIP if lin else ASKIP
            last = MN if lin else AN

            def puts_at(at):
                return puts and skip <= at - 2 < last

            if order is not None:
                nc.gpsimd.iota(rec[:, :, OWN:OWN + 1], [[P, GT]], base=order * GT * P, channel_multiplier=1).then_inc(S("ids_drawn"), 1)
            if order is not None and ASKIP:
                order_records()
                load_records()
            if not transform:
                def body(step, i, b, at):
                    put = puts_at(at)
                    parts_left = gather(step, i, b) if attends(at) else None
                    if parts_left:
                        next(parts_left)
                    if lin and put:
                        scatter(step - 2, i - 1, b, skip)
                    if parts_left:
                        for _ in parts_left:
                            pass
                    if layer == 1 and put:
                        scatter(step - 2, i - 1, b, skip)
                    if at == LAG - 3 and not ASKIP and order is not None:
                        order_records()
                    if at == LAG - 2 and not ASKIP and order is not None:
                        load_records()

                steps(pool, body)
                for step in range(STEPS, STEPS + 2):
                    if puts and step - 2 < last:
                        scatter(step - 2, step // 2 - 1, step % 2, skip)
                if puts:
                    for b in range(2):
                        pool.wait_ge(S(f"out_scattered{b}"), 16 * ((last - skip) // 2))

        @block.vector
        def _(dve):
            if scan is not None:
                dve.sem_inc(S("picked"), 2)
                dve.sem_inc(S("listed"), 1)

            def listing(n, step, b):
                at = 1 + OPS * step + n
                flat = cand[:, b].rearrange("p b k -> p (b k)")
                m = n - 1
                if n == 0:
                    dve.wait_ge(S("picked"), 2 + HALVES * step)
                    nc.vector.reduce_max(crowded[:, bass.ds(step, 1)], cand[:, b, :, CAND - 1], AX_X).then_inc(S("listed"), 1)
                elif n == OPS - 1:
                    dve.wait_ge(S("listed"), at)
                    nc.vector.tensor_copy(keys[:, bass.ds(step, 1), :].rearrange("p o k -> p (o k)"), top[:]).then_inc(S("listed"), 1)
                else:
                    dve.wait_ge(S("listed"), at)
                    dve.nop(nofuse=True)
                    left = flat if m < 2 else rest[:, (m // 2 - 1) % 2, :]
                    best = top[:, m // 2 * CAND:(m // 2 + 1) * CAND]
                    if m % 2 == 0:
                        nc.vector.max(best, left).then_inc(S("listed"), 1)
                    else:
                        nc.vector.match_replace(rest[:, m // 2 % 2, :], best, left, imm_value=-2.0 * N).then_inc(S("listed"), 1)

            def transforming(n, step, i, b):
                if n in (0, 1):
                    if n == 0:
                        dve.wait_ge(S(f"x_loaded{b}"), 16 * i + 16)
                    for q in (2 * n, 2 * n + 1):
                        nc.vector.bn_stats(stats[:, q, :], x_in[:, b, q, 0:D]).then_inc(S("stat"), 1)
                elif n in (2, 3):
                    dve.wait_ge(S("stat"), Q * step + 2 * (n - 1))
                    dve.nop(nofuse=True)
                    for q in (2 * n - 4, 2 * n - 3):
                        nc.vector.bn_aggr(mv[:, q, :], stats[:, q, :]).then_inc(S("aggr"), 1)
                elif n == 6:
                    dve.wait_ge(S("rooted"), step + 1)
                    nc.vector.reciprocal(rstd[:], std[:]).then_inc(S("inverted"), 1)
                elif n in (7, 8):
                    dve.wait_ge(S("inverted"), step + 1)
                    dve.wait_ge(S("turned"), step + 1)
                    for q in (2 * n - 14, 2 * n - 13):
                        op = nc.vector.tensor_scalar(x_hat[:, q, :], x_in[:, b, q, 0:D], mv[:, q, 0:1], rstd[:, q:q + 1],
                                                     ALU.subtract, ALU.mult)
                    if n == 8:
                        op.then_inc(S("normed"), 1)

            OWN_STEPS = 7
            FIN_STEPS = 4 if layer == 0 else 1

            def attending(n, step, i, b, at):
                here = step - ASKIP
                done = OWN_STEPS * here
                a = step + A0
                deg = all_f[:, bass.ds(a, 1), DEG:DEG + 1].rearrange("p o d -> p (o d)")
                own_s1 = all_f[:, bass.ds(a, 1), OWN_S1:OWN_S1 + 1].rearrange("p o d -> p (o d)")
                own_x = all_f[:, bass.ds(a, 1), OWN_X:OWN_X + D].rearrange("p o d -> p (o d)")
                if n == 0:
                    dve.wait_ge(S("near_ready"), here + 1)
                    nc.vector.tensor_scalar(e[:], near[b][:, :, S2], own_s1, None, ALU.add).then_inc(S("step"), 1)
                    nc.vector.tensor_scalar(pen[:], slot[:], deg, BIG, ALU.is_lt, ALU.mult).then_inc(S("step"), 1)
                elif n == 1:
                    dve.wait_ge(S("step"), done + 1)
                    nc.vector.scalar_tensor_tensor(e[:], e[:], ALPHA, e[:], ALU.mult, ALU.max).then_inc(S("step"), 1)
                elif n == 2:
                    dve.wait_ge(S("step"), done + 3)
                    nc.vector.scalar_tensor_tensor(e[:], pen[:], NEG, e[:], ALU.add, ALU.min).then_inc(S("step"), 1)
                elif n == 3:
                    dve.wait_ge(S("step"), done + 4)
                    nc.vector.tensor_reduce(neg_max[:], e[:], AX_X, ALU.max, negate=True).then_inc(S("max_ready"), 1)
                elif n == 4:
                    nc.vector.tensor_scalar(alone[:, b:b + 1], deg, 0.0, None, ALU.is_equal).then_inc(S("step"), 1)
                elif n == 5:
                    dve.wait_ge(S("exp_ready"), here + 1)
                    dve.wait_ge(S("step"), done + 5)
                    nc.vector.scalar_tensor_tensor(p[:], slot[:], deg, p_all[:], ALU.is_lt, ALU.mult, accum_out=den[:]).then_inc(S("p_ready"), 1)
                elif n == 6:
                    dve.wait_ge(S("p_ready"), here + 1)
                    nc.vector.tensor_scalar(den[:], den[:], alone[:, b:b + 1], None, ALU.add).then_inc(S("step"), 1)
                elif n == 7:
                    dve.wait_ge(S("step"), done + 6)
                    nc.vector.reciprocal(rden[:, b:b + 1], den[:]).then_inc(S("step"), 1)
                elif n == 10:
                    if at + 2 < AN:
                        indices(step + 2, b, at)

            def finishing(n, step, i, b):
                here = step - ASKIP
                done = FIN_STEPS * here
                a = step + A0
                own_x = all_f[:, bass.ds(a, 1), OWN_X:OWN_X + D].rearrange("p o d -> p (o d)")
                if n == 8:
                    dve.wait_ge(S("summed"), here + 2)
                    dve.wait_ge(S("step"), OWN_STEPS * (here + 1))
                    nc.vector.tensor_scalar(o[:], ps_o[:, 0:D], rden[:, b:b + 1], None, ALU.mult).then_inc(S("o_ready"), 1)
                elif n == 9:
                    dve.wait_ge(S("o_ready"), here + 2)
                    if layer == 1:
                        stored(dve, i, b, ASKIP)
                        nc.vector.tensor_copy(out_idx[:, b:b + 1], rec_all[:].bitcast(U32)[:, bass.ds(a, 1), OWN:OWN + 1].rearrange("p o d -> p (o d)")).then_inc(S("fin_ready"), 1)
                    nc.vector.scalar_tensor_tensor(res[:], o[:], 0.0, own_x, ALU.max, ALU.add).then_inc(S("fin_step"), 1)
                elif n == 14:
                    dve.wait_ge(S("ex_ready"), here + 1)
                    dve.wait_ge(S("fin_step"), done + 1)
                    dst = fin[:, b, :] if layer == 1 else own_x
                    nc.vector.scalar_tensor_tensor(dst, ex[:], -1.0, res[:], ALU.add, ALU.add).then_inc(S("fin_ready"), 1)
                elif n == 15 and layer == 0:
                    dve.wait_ge(S("fin_ready"), here + 1)
                    dve.nop(nofuse=True)
                    nc.vector.bn_stats(st[:], own_x).then_inc(S("fin_step"), 1)
                elif n == 16 and layer == 0:
                    dve.wait_ge(S("fin_step"), done + 2)
                    dve.nop(nofuse=True)
                    nc.vector.bn_aggr(mv1[:], st[:]).then_inc(S("fin_step"), 1)
                    dve.wait_ge(S("fin_step"), done + 3)
                    nc.vector.tensor_copy(mv_all[:, bass.ds(a, 1), :].rearrange("p o d -> p (o d)"), mv1[:]).then_inc(S("fin_step"), 1)

            def indices(step, b, at):
                if order is not None and at is not None and at + 2 == LAG:
                    dve.wait_ge(S("rec_loaded"), 16)
                nc.vector.tensor_copy(idx[b][:], rec_all[:].bitcast(U32)[:, bass.ds(step + A0, 1), 0:SLOTS].rearrange("p o k -> p (o k)")).then_inc(S("idx_ready"), 1)

            def normalizing(n, step, i, b):
                here = step - MSKIP
                m = step + M0
                if n == 1:
                    dve.wait_ge(S("l_turned"), here + 1)
                    stored(dve, i, b, MSKIP)
                    own_x = all_f[:, bass.ds(m, 1), OWN_X:OWN_X + D].rearrange("p o d -> p (o d)")
                    mean = mv_all[:, bass.ds(m, 1), 0:1].rearrange("p o d -> p (o d)")
                    nc.vector.tensor_copy(out_idx[:, b:b + 1], rec_all[:].bitcast(U32)[:, bass.ds(m, 1), OWN:OWN + 1].rearrange("p o d -> p (o d)")).then_inc(S("l_named"), 1)
                    nc.vector.tensor_scalar(x_hat1[:, b, :], own_x, mean, rstd_all[:, bass.ds(m, 1)], ALU.subtract, ALU.mult).then_inc(S("l_normed"), 1)

            def order_rows():
                chain = [0]
                step = S("o_step")

                def link(op):
                    chain[0] += 1
                    op.then_inc(step, 1)
                    dve.wait_ge(step, chain[0])

                got = keys[:, 1:GT + 1, :]
                link(nc.vector.tensor_scalar(valid[:], got, float(N), None, ALU.is_ge))
                link(nc.vector.reduce_sum(degree[:], valid[:], AX_X))
                link(nc.vector.tensor_scalar(bounded[:], degree[:], float(SLOTS - 1), None, ALU.min))
                nc.vector.tensor_tensor(member[:], const["falling"][:].unsqueeze(2).to_broadcast([P, SLOTS, GT]),
                                        bounded[:].unsqueeze(1).to_broadcast([P, SLOTS, GT]), ALU.is_equal).then_inc(S("member_ready"), 1)
                link(nc.vector.scalar_tensor_tensor(far[:], valid[:], -FAR, got, ALU.mult, ALU.add))
                link(nc.vector.tensor_scalar(rec[:, :, 0:SLOTS], far[:], FAR - N, None, ALU.add))
                link(nc.vector.tensor_copy(rec_f[:, :, DEG], degree[:]))
                dve.wait_ge(S("counted"), 1)
                one = const["one"]
                link(nc.vector.tensor_tensor_scan(upto[:], one[:].to_broadcast([P, SLOTS * GT]), ps_lin[:, 1, :SLOTS * GT], 0.0, ALU.mult, ALU.add))
                link(nc.vector.tensor_tensor(upto_own[:], upto[:], ps_lin[:, 0, :SLOTS * GT], ALU.subtract))
                link(nc.vector.tensor_tensor(upto_own[:], upto_own[:], member[:].rearrange("p c t -> p (c t)"), ALU.mult))
                link(nc.vector.reduce_sum(rank[:], upto_own[:].rearrange("p (c t) -> p t c", t=GT), AX_X))
                nc.vector.tensor_scalar(rank_i[:], rank[:], float(order * GT * P), None, ALU.add).then_inc(S("ranked"), 1)
                link(nc.vector.tensor_tensor(above[:], upto[0:1, :].rearrange("p (c t) -> p t c", t=GT)[:, GT - 1:GT, 0:SLOTS - 1].to_broadcast([1, GT, SLOTS - 1]),
                                             const["first_row"][:].unsqueeze(2).to_broadcast([1, GT, SLOTS - 1]), ALU.is_gt))
                mine = head[0:1, order * GT:(order + 1) * GT]
                link(nc.vector.reduce_sum(mine, above[:], AX_X))
                link(nc.vector.tensor_scalar(mine, mine, float(W4), None, ALU.max))
                link(nc.vector.tensor_copy(count_of[0:1, order * GT:(order + 1) * GT], mine))
                dve.sem_inc(S("counts_ready"), 1)
                link(nc.vector.reduce_max(most[:, 0:1], crowded[:, 1:GT + 1], AX_X))
                link(nc.vector.reduce_max(most[:, 1:2], degree[:], AX_X))
                link(nc.vector.tensor_scalar(most[:, 2:3], most[:, 0:1], float(N), None, ALU.is_ge))
                link(nc.vector.tensor_scalar(const["over"][:, order:order + 1], most[:, 1:2], float(SLOTS), most[:, 2:3], ALU.is_ge, ALU.max))

            def take():
                lo, hi = A0 + ASKIP, A0 + AN
                n = hi - lo
                ts = S("taken_step")
                nc.vector.tensor_scalar(taken[0:1, 0:n], head[0:1, lo:hi], 16.0, None, ALU.mult).then_inc(ts, 1)
                dve.wait_ge(ts, 1)
                for b in range(2):
                    nc.vector.tensor_tensor_scan(taken_sum[0:1, b:n:2], const["one"][0:1, :].to_broadcast([1, n // 2]),
                                                 taken[0:1, b:n:2], 0.0, ALU.mult, ALU.add).then_inc(ts, 1)
                dve.wait_ge(ts, 3)
                nc.vector.tensor_copy(taken_of[0:1, lo:hi], taken_sum[0:1, 0:n]).then_inc(S("taken_ready"), 1)

            if transform:
                nc.vector.memset(rows[:], 1.0).then_inc(S("padded"), 1)
                nc.vector.memset(x_in[:, :, :, D:ROW], 0.0).then_inc(S("padded"), 1)
            if attend and not ASKIP:
                for b in range(2):
                    indices(b, b, None)
            if order is not None:
                order_rows()
            if attend:
                take()
            if lin:
                dve.wait_ge(S("l_rooted"), 1)
                nc.vector.reciprocal(rstd_all[:, M0 + MSKIP:M0 + MN], std_all[:, MSKIP:MN]).then_inc(S("l_inverted"), 1)
                dve.wait_ge(S("l_inverted"), 1)

            def body(step, i, b, at):
                for n in range(17):
                    if scan is not None and n < NBLK:
                        if n % BANKS == 0:
                            h = n // BANKS
                            dve.wait_ge(S("keyed"), HALVES * step + h + 1)
                            dve.nop(nofuse=True)
                        op = nc.vector.max(cand[:, b, n, :], ps_keys[h % 2][:, n % BANKS, :])
                        if n % BANKS == BANKS - 1:
                            op.then_inc(S("picked"), 1)
                    if scan is not None and n < OPS:
                        listing(n, step, 1 - b)
                    if transform:
                        transforming(n, step, i, b)
                    if attends(at - 1):
                        finishing(n, step - 1, i if b else i - 1, 1 - b)
                    if attends(at):
                        attending(n, step, i, b, at)
                    elif n == 10 and attend and ASKIP <= at + 2 < AN:
                        indices(step + 2, b, at)
                    if lins(at):
                        normalizing(n, step, i, b)

            steps(dve, body)
            if attends(STEPS - 1):
                for n in range(8, 17):
                    finishing(n, STEPS - 1, STEPS // 2 - 1, 1)
            if scan is not None:
                for n in range(OPS):
                    listing(n, STEPS, 1)
            if transform or close:
                dve.wait_ge(S("relued" if transform else "l_relued"), GT if transform else MN - MSKIP + 1)
                width = GT if transform else NT
                nc.vector.reduce_sum(h_sum[:], h_sums[:, 0:width], AX_X).then_inc(S("h_summed"), 1)
                dve.wait_ge(S("h_summed"), 1)
                nc.vector.tensor_copy(h_sum_wide[:], h_sum[:].to_broadcast([P, P])).then_inc(S("h_widened"), 1)
                dve.wait_ge(S("averaged"), 1)
                nc.vector.tensor_scalar(mean_wh[:], ps_o[:, 0:D], 1.0 / N, None, ALU.mult).then_inc(S("mean_ready"), 1)
            if close:
                nc.vector.reduce_max(flag[:], const["over"][:], AX_X).then_inc(S("flagged"), 1)
                dve.wait_ge(S("flags_summed"), 1)
                nc.vector.tensor_copy(const["overflow"][:], ps_h[0:1, 0:1]).then_inc(S("overflow_ready"), 1)

        @block.scalar
        def _(act):
            if attend:
                act.sem_inc(S("parts_ready"), 2)
            if lin:
                act.sem_inc(S("l_ready"), 2)
            if lin:
                nc.scalar.activation(std_all[:, MSKIP:MN], mv_all[:, M0 + MSKIP:M0 + MN, 1], ACT.Sqrt, bias=eps[:, 0:1]).then_inc(S("l_rooted"), 1)
            if scan is not None:
                act.sem_inc(S("edge_ready"), NCH)

            def sign(step, c):
                act.wait_ge(S(f"adj_loaded{c}"), 16 * step + 16)
                nc.scalar.activation(edge[:, c, :], adj_in[:, c, :], ACT.Sign).then_inc(S("edge_ready"), 1)

            if scan is not None:
                for c in range(NCH):
                    sign(0, c)
            def row(step, i, b):
                there = step - MSKIP
                act.wait_ge(S("l_multiplied"), there + 2)
                stored(act, i, b, MSKIP)
                nc.scalar.activation(lin_rows[:, b, 0:AUG], ps_lin[:, 1, 0:AUG], ACT.Copy).then_inc(S("l_ready"), 1)
                nc.scalar.activation(all_f[:, bass.ds(step + M0, 1), OWN_S1:OWN_S1 + 1].rearrange("p o d -> p (o d)"),
                                     ps_lin[:, 1, S1:S1 + 1], ACT.Copy).then_inc(S("l_ready"), 1)

            def grow(here):
                act.wait_ge(S("o_ready"), here + 2)
                nc.scalar.activation(low[:], o[:], ACT.Relu, scale=-1.0).then_inc(S("low_ready"), 1)
                act.wait_ge(S("low_ready"), here + 1)
                nc.scalar.activation(ex[:], low[:], ACT.Exp, scale=-1.0).then_inc(S("ex_ready"), 1)

            def body(step, i, b, at):
                def next_sign(c):
                    if scan is not None and at + 1 < GT:
                        act.wait_ge(S("keyed"), HALVES * step + HPC * (c + 1))
                        sign(step + 1, c)

                here = step - ASKIP
                there = step - MSKIP
                a, m = step + A0, step + M0
                if transform:
                    act.wait_ge(S("aggr"), Q * step + Q)
                    nc.scalar.activation(std[:], mv[:, :, 1], ACT.Sqrt, bias=eps[:, 0:1]).then_inc(S("rooted"), 1)
                next_sign(0)
                if lins(at):
                    act.wait_ge(S("l_turned"), there + 3)
                    act.wait_ge(S("l_multiplied"), there + 1)
                    nc.scalar.activation(h_t1[:, b, :], ps_lin[:, 0, 0:D], ACT.Relu, accum_out=h_sums[:, bass.ds(m, 1)]).then_inc(S("l_relued"), 1)
                if attends(at):
                    act.wait_ge(S("max_ready"), here + 1)
                    nc.scalar.activation(p_all[:], e[:], ACT.Exp, bias=neg_max[:, 0:1]).then_inc(S("exp_ready"), 1)
                next_sign(1)
                if attends(at):
                    if order is not None and at == LAG:
                        act.wait_ge(S("counts_ready"), 1)
                    count = act.value_load(count_of[0:1, bass.ds(a, 1)], min_val=0, max_val=SLOTS)
                    act.wait_ge(S("p_ready"), here + 1)
                    act.wait_ge(S("summed"), here + 1)

                    def weigh(k):
                        for j in range(k, k + W2):
                            nc.scalar.activation(parts[:, j, :], near[b][:, j, 0:D], ACT.Copy, scale=p[:, j:j + 1])
                        if k + W2 < SLOTS:
                            with act.If(count > k + W2):
                                weigh(k + W2)

                    weigh(0)
                    nc.scalar.activation(base[:], mean_wh[:], ACT.Copy, scale=alone[:, b:b + 1]).then_inc(S("parts_ready"), 1)
                if attends(at - 1):
                    grow(here - 1)
                if NCH > 2:
                    next_sign(2)
                if transform:
                    act.wait_ge(S("turned"), step + 2)
                    nc.scalar.activation(h_t[:], ps_h[:].rearrange("p (q n) -> p q n", q=Q), ACT.Relu, accum_out=h_sums[:, bass.ds(step, 1)]).then_inc(S("relued"), 1)
                if NCH > 3:
                    next_sign(3)
                if lins(at):
                    row(step, i, b)
                if transform:
                    wide = ps_lin[:].rearrange("p a (h w) -> p (a h) w", w=256)
                    act.wait_ge(S("multiplied"), step + 1)
                    act.wait_ge(S("row_free"), step + 1)
                    nc.scalar.activation(rows[:, b, :, 0:AUG], wide[:, :, 0:AUG], ACT.Copy).then_inc(S("row_ready"), 1)
                    nc.scalar.activation(x_in[:, b, :, D:D + 1], wide[:, :, S1:S1 + 1], ACT.Copy).then_inc(S("row_ready"), 1)

            steps(act, body)
            if attends(STEPS - 1):
                grow(STEPS - 1 - ASKIP)

        @block.tensor
        def _(pe):
            if order is not None:
                flat = member[:].rearrange("p c t -> p (c t)")
                pe.wait_ge(S("member_ready"), 1)
                nc.tensor.matmul(ps_lin[:, 0, :SLOTS * GT], const["after"][:], flat, start=True, stop=True)
                nc.tensor.matmul(ps_lin[:, 1, :SLOTS * GT], const["ones_bf"][:], flat, start=True, stop=True).then_inc(S("counted"), 1)
            if attend:
                pe.sem_inc(S("summed"), 1)
                pe.sem_inc(S("o_ready"), 1)
            if transform:
                pe.sem_inc(S("turned"), 1)
            if lin:
                pe.sem_inc(S("l_turned"), 2)
                pe.sem_inc(S("l_multiplied"), 1)
                pe.sem_inc(S("l_relued"), 1)

            def product(step, b):
                there = step - MSKIP
                pe.wait_ge(S("l_relued"), there + 2)
                pe.wait_ge(S("l_ready"), 2 * there + 2)
                nc.tensor.matmul(ps_lin[:, 1, 0:AUG], h_t1[:, b, :], waug[:, 1, :], start=True, stop=True).then_inc(S("l_multiplied"), 1)

            def count_at(step, at):
                if order is not None and at == LAG:
                    pe.wait_ge(S("counts_ready"), 1)
                return pe.value_load(count_of[0:1, bass.ds(step + A0, 1)], min_val=0, max_val=SLOTS)

            def add(turn, count, here):
                def group(k, end):
                    for j in range(k, k + W2):
                        nc.tensor.matmul(ps_o[:, 0:D], ident[:], parts[:, j, :], start=j == 0, stop=False)
                    if k + W2 < end:
                        with pe.If(count > k + W2):
                            group(k + W2, end)

                if turn == 0:
                    pe.wait_ge(S("parts_ready"), here + 3)
                    pe.wait_ge(S("o_ready"), here + 1)
                    group(0, W4)
                else:
                    with pe.If(count > turn * W4):
                        group(turn * W4, SLOTS if turn == TURNS - 1 else (turn + 1) * W4)
                if turn == TURNS - 1:
                    nc.tensor.matmul(ps_o[:, 0:D], ident[:], base[:], start=False, stop=True).then_inc(S("summed"), 1)

            def body(step, i, b, at):
                here = step - ASKIP
                there = step - MSKIP
                if attends(at - 1):
                    count = count_at(step - 1, at - 1)
                for h in range(HALVES):
                    c = h // HPC
                    if scan is not None:
                        pe.wait_ge(S("picked"), HALVES * step + h + 1)
                        for w in range(BANKS):
                            k = h * BANKS + w
                            nc.tensor.matmul(ps_keys[h % 2][:, w, :], const["ones_bf"][:], const["col"][:, k * BW:(k + 1) * BW],
                                             start=True, stop=False)
                        if h % HPC == 0:
                            pe.wait_ge(S("edge_ready"), NCH + NCH * step + c + 1)
                        for w in range(BANKS):
                            k = (h % HPC) * BANKS + w
                            op = nc.tensor.matmul(ps_keys[h % 2][:, w, :], const["lift"][:], edge[:, c, k * BW:(k + 1) * BW],
                                                  start=False, stop=True)
                        op.then_inc(S("keyed"), 1)
                    if transform and h == 5 * HALVES // 8:
                        pe.wait_ge(S("normed"), step + 1)
                        for q in range(Q):
                            op = nc.tensor.transpose(ps_h[:, q * P:(q + 1) * P], x_hat[:, q, :], ident[:])
                        op.then_inc(S("turned"), 1)
                    if attends(at - 1) and h < TURNS:
                        add(h, count, here - 1)
                    if lins(at) and h == 1:
                        pe.wait_ge(S("l_normed"), there + 1)
                        pe.wait_ge(S("l_relued"), there + 1)
                        nc.tensor.transpose(ps_lin[:, 0, 0:D], x_hat1[:, b, :], ident[:]).then_inc(S("l_turned"), 1)
                if transform:
                    pe.wait_ge(S("relued"), step + 1)
                    wide = ps_lin[:].rearrange("p a (h w) -> p (a h) w", w=256)
                    for q in range(Q):
                        op = nc.tensor.matmul(wide[:, q, 0:AUG], h_t[:, q, :], waug[:, 0, :], start=True, stop=True)
                    op.then_inc(S("multiplied"), 1)
                if lins(at):
                    product(step, b)

            steps(pe, body)
            if attends(STEPS - 1):
                count = count_at(STEPS - 1, STEPS - 1)
                for turn in range(TURNS):
                    add(turn, count, STEPS - 1 - ASKIP)
            if transform or close:
                pe.wait_ge(S("h_widened"), 1)
                nc.tensor.matmul(ps_o[:, 0:D], h_sum_wide[:], waug[:, 0 if transform else 1, 0:D], start=True, stop=True).then_inc(S("averaged"), 1)
            if close:
                pe.wait_ge(S("flagged"), 1)
                nc.tensor.matmul(ps_h[0:1, 0:1], flag[:], const["one"][:], start=True, stop=True).then_inc(S("flags_summed"), 1)
    finish(nc, s)


def gat_kernel(nc, x, adj, W0, a0, W1, a1, out):
    N = x.shape[0]
    NT = N // P
    GT = NT // GROUPS
    table = [nc.dram_tensor(f"table{l}", [N, ROW], F32, kind="Internal").ap() for l in range(2)]
    s2_line = [nc.dram_tensor(f"s2_line{l}", [1, N], F32, kind="Internal").ap() for l in range(2)]
    self_rows = nc.dram_tensor("self_rows", [N, ROW], F32, kind="Internal").ap()
    x_mid = nc.dram_tensor("x_mid", [N, D], F32, kind="Internal").ap()
    records = nc.dram_tensor("records", [N, REC], I32, kind="Internal").ap()
    with ExitStack() as ctx:
        def sb(name, shape, dt=F32):
            return ctx.enter_context(nc.sbuf_tensor(name, shape, dt))

        const = {
            "ident": sb("ident", [P, P]),
            "waug": sb("waug", [P, 2, AUG]),
            "eps": sb("eps", [P, 1]),
            "mean_wh": sb("mean_wh", [P, D]),
            "slot": sb("slot", [P, SLOTS]),
            "overflow": sb("overflow", [1, 1], I32),
            "signals": [],
        }
        weights_stage(nc, const, [W0, W1], [a0, a1])
        with ExitStack() as fast:
            def fb(name, shape, dt=F32):
                const[name] = fast.enter_context(nc.sbuf_tensor(name, shape, dt))

            def bank(name, shape):
                return fast.enter_context(nc.psum_tensor(name, shape, F32))

            fb("col", [P, N], BF16)
            fb("lift", [P, P], BF16)
            fb("ones_bf", [P, P], BF16)
            fb("after", [P, P], BF16)
            fb("one", [P, 1])
            fb("falling", [P, SLOTS])
            fb("first_row", [1, GT])
            fb("adj_in", [P, N // CW, CW], I32)
            fb("edge", [P, N // CW, CW], BF16)
            fb("cand", [P, 2, N // BW, CAND])
            fb("keys", [P, GT + 1, SLOTS])
            fb("crowded", [P, GT + 1])
            fb("over", [P, GROUPS])
            fb("rec", [P, GT, REC], I32)
            fb("rec_all", [P, NT, REC], I32)
            fb("count_of", [1, NT], I32)
            fb("head", [1, NT])
            fb("taken_of", [1, NT], I32)
            fb("mv_all", [P, NT, 2])
            fb("rstd_all", [P, NT])
            fb("h_sums", [P, NT])
            fb("lin_rows", [P, 2, ROW])
            const["near"] = [fast.enter_context(nc.sbuf_tensor(f"near{b}", [P, SLOTS, ROW], F32)) for b in range(2)]
            const["ps_keys"] = [bank(f"ps_keys{b}", [P, BANKS, BW]) for b in range(2)]
            const["ps_o"] = bank("ps_o", [P, 512])
            const["ps_h"] = bank("ps_h", [P, 512])
            const["ps_lin"] = bank("ps_lin", [P, 2, 512])
            constants_stage(nc, const, N)

            def stage(name, **parts):
                pipeline_stage(nc, const, name, x, adj, table, self_rows, records, out, **parts)

            stage("s0", scan=0, transform=True)
            for g in range(1, GROUPS):
                first = (g - 1) * GT - LAG
                stage(f"s{g}", scan=g, order=g - 1,
                      attend=(0, (first, LAG if g == 1 else 0), GT),
                      lin=(first - GT, LAG if g == 2 else 0, GT) if g >= 2 else None)
            stage("drain", order=GROUPS - 1, attend=(0, ((GROUPS - 1) * GT - LAG, 0), GT + LAG),
                  lin=((GROUPS - 2) * GT - LAG, 0, GT))
            stage("close", lin=((GROUPS - 1) * GT - LAG, 0, GT + LAG), close=True)
            stage("layer1", attend=(1, (0, 0), NT))
        nc.clear_and_free_semaphores(const["signals"])
        nc.all_engine_barrier()
        const["signals"] = []
        flag = const["overflow"]
        node_transform(nc, const, 0, x, table[0], self_rows, s2_line[0], flag)
        dense_attention(nc, const, 0, table[0], s2_line[0], adj, x, x_mid, flag)
        node_transform(nc, const, 1, x_mid, table[1], self_rows, s2_line[1], flag)
        dense_attention(nc, const, 1, table[1], s2_line[1], adj, x_mid, out, flag)


_INS = ["x", "adj", "L0_gnn_W", "L0_gnn_a", "L1_gnn_W", "L1_gnn_a"]


def kernel(**inputs):
    import numpy as _np
    import concourse.bacc as _bacc
    from concourse import mybir as _mybir
    from concourse.bass_utils import run_bass_kernel_spmd as _run

    nc = _bacc.Bacc("TRN2", target_bir_lowering=False, num_devices=1)
    arrays, args = {}, []
    for name in _INS:
        a = _np.ascontiguousarray(inputs[name])
        arrays[f"in_{name}"] = a
        args.append(nc.dram_tensor(f"in_{name}", a.shape, _mybir.dt.from_np(a.dtype), kind="ExternalInput").ap())
    out = nc.dram_tensor("out", inputs["x"].shape, _mybir.dt.float32, kind="ExternalOutput").ap()
    gat_kernel(nc, *args, out)
    r = _run(nc, [arrays], core_ids=[0])
    return r.results[0]["out"]
```
